# Optimizing a Trainium2 kernel written in Bass

```python
import numpy as np
import jax
import jax.numpy as jnp

def _softmax(x, axis=-1):
    return jax.nn.softmax(x, axis=axis)
def _gelu(x):
    return jax.nn.gelu(x, approximate=True)
def _silu(x):
    return jax.nn.silu(x)
def _sigmoid(x):
    return jax.nn.sigmoid(x)
def _layernorm(x, axis=-1, eps=1e-5):
    m = jnp.mean(x, axis=axis, keepdims=True)
    v = jnp.var(x, axis=axis, keepdims=True)
    return (x - m) / jnp.sqrt(v + eps)
def _scatter_add(tgt, idx, src, axis=0):
    return tgt.at[idx].add(src)
def _segment_sum(src, seg, n):
    return jax.ops.segment_sum(src, seg, n)

kernel_name = 'mk_conv_seq_d2_conv_nchw64_1c07f4'

def setup_inputs(seed: int = 0):
    np.random.seed(seed)
    _w = jnp.asarray
    def _rec_inputs():
        import jax
        import jax.numpy as jnp
        _gk = jax.random.key(seed)
        x = 7.22e-05 + 1 * jax.random.normal(jax.random.fold_in(_gk, 1), (8, 64, 128, 128), jnp.float32)
        return x
    x = _rec_inputs()
    def _L0_conv_setup():
        import jax, jax.numpy as jnp
        from jax import lax
        import numpy as np
        D_STATE = 16
        D_CONV = 4
        GN_EPS = 1e-05

        def silu(x):
            return x * jax.nn.sigmoid(x)

        def causal_conv(x, w, b):
            xc = jnp.transpose(x, (0, 2, 1))
            y = lax.conv_general_dilated(xc, w, (1,), [(D_CONV - 1, 0)], feature_group_count=w.shape[0], dimension_numbers=('NCH', 'OIH', 'NCH'))
            y = y + b[None, :, None]
            return jnp.transpose(y, (0, 2, 1))

        def selective_scan(u, delta, A, Bm, Cm, D):

            def step(h, inp):
                u_t, d_t, B_t, C_t = inp
                dA = jnp.exp(d_t[..., None] * A)
                h = dA * h + (d_t * u_t)[..., None] * B_t[:, None, :]
                y = jnp.einsum('bdn,bn->bd', h, C_t)
                return (h, y)
            h0 = jnp.zeros((u.shape[0], A.shape[0], A.shape[1]), u.dtype)
            xs = (jnp.transpose(u, (1, 0, 2)), jnp.transpose(delta, (1, 0, 2)), jnp.transpose(Bm, (1, 0, 2)), jnp.transpose(Cm, (1, 0, 2)))
            _, ys = lax.scan(step, h0, xs)
            return jnp.transpose(ys, (1, 0, 2)) + u * D

        def mamba(seq, p):
            in_w, conv_w, conv_b, xp_w, dt_w, dt_b, A_log, Dp, out_w = p
            di = in_w.shape[0] // 2
            xz = jnp.einsum('blc,ec->ble', seq, in_w)
            x, z = (xz[..., :di], xz[..., di:])
            x = silu(causal_conv(x, conv_w, conv_b))
            xdbl = jnp.einsum('bld,ed->ble', x, xp_w)
            dtr = dt_w.shape[1]
            dt = xdbl[..., :dtr]
            Bm = xdbl[..., dtr:dtr + D_STATE]
            Cm = xdbl[..., dtr + D_STATE:]
            delta = jax.nn.softplus(jnp.einsum('blr,dr->bld', dt, dt_w) + dt_b)
            A = -jnp.exp(A_log)
            y = selective_scan(x, delta, A, Bm, Cm, Dp)
            y = y * silu(z)
            return jnp.einsum('bld,cd->blc', y, out_w)

        def run_bidir(seq, p):
            f = mamba(seq, p)
            r = jnp.flip(mamba(jnp.flip(seq, 1), p), 1)
            return 0.5 * (f + r)

        def _mamba_params(key, c):
            di = 2 * c
            dtr = max(1, -(-c // 16))
            ks = jax.random.split(key, 7)
            in_w = jax.random.normal(ks[0], (2 * di, c), jnp.float32) * 0.02
            conv_w = jax.random.normal(ks[1], (di, 1, D_CONV), jnp.float32) * 0.1
            conv_b = jnp.zeros((di,), jnp.float32)
            xp_w = jax.random.normal(ks[2], (dtr + 2 * D_STATE, di), jnp.float32) * 0.02
            dt_w = jax.random.normal(ks[3], (di, dtr), jnp.float32) * 0.1
            dt_b = jax.random.normal(ks[4], (di,), jnp.float32) * 0.1 - 4.0
            A_log = jnp.log(jnp.broadcast_to(jnp.arange(1.0, D_STATE + 1.0, dtype=jnp.float32), (di, D_STATE)))
            Dp = jnp.ones((di,), jnp.float32)
            out_w = jax.random.normal(ks[5], (c, di), jnp.float32) * 0.02
            return (in_w, conv_w, conv_b, xp_w, dt_w, dt_b, A_log, Dp, out_w)
        key = jax.random.key(seed)
        b, c, h, w = (8, 64, 128, 128)
        kx, kr, kc, kg = jax.random.split(key, 4)
        x = jax.random.normal(kx, (b, c, h, w), jnp.float32)
        rp = _mamba_params(kr, c)
        cp = _mamba_params(kc, c)
        names = ('in_w', 'conv_w', 'conv_b', 'xp_w', 'dt_w', 'dt_b', 'A_log', 'D', 'out_w')
        d = {'x': x}
        for n, v in zip(names, rp):
            d['row_' + n] = v
        for n, v in zip(names, cp):
            d['col_' + n] = v
        d['gn_w'] = jnp.ones((c,), jnp.float32)
        d['gn_b'] = jnp.zeros((c,), jnp.float32)
        return d
    _L0_conv_all = _L0_conv_setup()
    _L0_conv_in = {k: v for k, v in _L0_conv_all.items() if k in ('row_in_w', 'row_conv_w', 'row_conv_b', 'row_xp_w', 'row_dt_w', 'row_dt_b', 'row_A_log', 'row_D', 'row_out_w', 'col_in_w', 'col_conv_w', 'col_conv_b', 'col_xp_w', 'col_dt_w', 'col_dt_b', 'col_A_log', 'col_D', 'col_out_w', 'gn_w', 'gn_b', )}
    del _L0_conv_all

    def _L1_conv_setup():
        import jax, jax.numpy as jnp
        import numpy as np
        from jax import lax
        KSHAPE = (64, 64, 3, 3)
        KSIZE = 64 * 64 * 9
        EPS = 1e-05

        def _conv3x3(x, w, stride):
            return lax.conv_general_dilated(x, w, window_strides=(stride, stride), padding=[(1, 1), (1, 1)], dimension_numbers=('NCHW', 'OIHW', 'NCHW'))

        def _batchnorm(x, gamma, beta):
            mean = jnp.mean(x, axis=(0, 2, 3), keepdims=True)
            var = jnp.var(x, axis=(0, 2, 3), keepdims=True)
            xhat = (x - mean) * lax.rsqrt(var + EPS)
            return xhat * gamma[None, :, None, None] + beta[None, :, None, None]
        key = jax.random.key(seed)
        ks = jax.random.split(key, 4)
        x = jax.random.normal(ks[0], (128, 64, 32, 32), dtype=jnp.float32)
        origin_weight = jax.random.normal(ks[1], (2 * KSIZE,), dtype=jnp.float32) * 0.05
        P_weight = jax.random.normal(ks[2], (40, 2 * KSIZE), dtype=jnp.float32) * 0.05
        new_param = jax.random.normal(ks[3], (40,), dtype=jnp.float32) * 0.1
        return {'x': x, 'origin_weight': origin_weight, 'P_weight': P_weight, 'new_param': new_param, 'bn1_gamma': jnp.ones((64,), jnp.float32), 'bn1_beta': jnp.zeros((64,), jnp.float32), 'bn2_gamma': jnp.ones((64,), jnp.float32), 'bn2_beta': jnp.zeros((64,), jnp.float32)}
    _L1_conv_all = _L1_conv_setup()
    _L1_conv_in = {k: v for k, v in _L1_conv_all.items() if k in ('origin_weight', 'P_weight', 'new_param', 'bn1_gamma', 'bn1_beta', 'bn2_gamma', 'bn2_beta', )}
    del _L1_conv_all

    return {
        "x": x,
        "L0_conv_row_in_w": _L0_conv_in["row_in_w"],
        "L0_conv_row_conv_w": _L0_conv_in["row_conv_w"],
        "L0_conv_row_conv_b": _L0_conv_in["row_conv_b"],
        "L0_conv_row_xp_w": _L0_conv_in["row_xp_w"],
        "L0_conv_row_dt_w": _L0_conv_in["row_dt_w"],
        "L0_conv_row_dt_b": _L0_conv_in["row_dt_b"],
        "L0_conv_row_A_log": _L0_conv_in["row_A_log"],
        "L0_conv_row_D": _L0_conv_in["row_D"],
        "L0_conv_row_out_w": _L0_conv_in["row_out_w"],
        "L0_conv_col_in_w": _L0_conv_in["col_in_w"],
        "L0_conv_col_conv_w": _L0_conv_in["col_conv_w"],
        "L0_conv_col_conv_b": _L0_conv_in["col_conv_b"],
        "L0_conv_col_xp_w": _L0_conv_in["col_xp_w"],
        "L0_conv_col_dt_w": _L0_conv_in["col_dt_w"],
        "L0_conv_col_dt_b": _L0_conv_in["col_dt_b"],
        "L0_conv_col_A_log": _L0_conv_in["col_A_log"],
        "L0_conv_col_D": _L0_conv_in["col_D"],
        "L0_conv_col_out_w": _L0_conv_in["col_out_w"],
        "L0_conv_gn_w": _L0_conv_in["gn_w"],
        "L0_conv_gn_b": _L0_conv_in["gn_b"],
        "L1_conv_origin_weight": _L1_conv_in["origin_weight"],
        "L1_conv_P_weight": _L1_conv_in["P_weight"],
        "L1_conv_new_param": _L1_conv_in["new_param"],
        "L1_conv_bn1_gamma": _L1_conv_in["bn1_gamma"],
        "L1_conv_bn1_beta": _L1_conv_in["bn1_beta"],
        "L1_conv_bn2_gamma": _L1_conv_in["bn2_gamma"],
        "L1_conv_bn2_beta": _L1_conv_in["bn2_beta"],
    }

def reference(x, L0_conv_row_in_w, L0_conv_row_conv_w, L0_conv_row_conv_b, L0_conv_row_xp_w, L0_conv_row_dt_w, L0_conv_row_dt_b, L0_conv_row_A_log, L0_conv_row_D, L0_conv_row_out_w, L0_conv_col_in_w, L0_conv_col_conv_w, L0_conv_col_conv_b, L0_conv_col_xp_w, L0_conv_col_dt_w, L0_conv_col_dt_b, L0_conv_col_A_log, L0_conv_col_D, L0_conv_col_out_w, L0_conv_gn_w, L0_conv_gn_b, L1_conv_origin_weight, L1_conv_P_weight, L1_conv_new_param, L1_conv_bn1_gamma, L1_conv_bn1_beta, L1_conv_bn2_gamma, L1_conv_bn2_beta):
    import jax
    import jax.numpy as jnp
    def _L0_conv_ref(x, row_in_w, row_conv_w, row_conv_b, row_xp_w, row_dt_w, row_dt_b, row_A_log, row_D, row_out_w, col_in_w, col_conv_w, col_conv_b, col_xp_w, col_dt_w, col_dt_b, col_A_log, col_D, col_out_w, gn_w, gn_b):
        import jax, jax.numpy as jnp
        from jax import lax
        import numpy as np
        D_STATE = 16
        D_CONV = 4
        GN_EPS = 1e-05

        def silu(x):
            return x * jax.nn.sigmoid(x)

        def causal_conv(x, w, b):
            xc = jnp.transpose(x, (0, 2, 1))
            y = lax.conv_general_dilated(xc, w, (1,), [(D_CONV - 1, 0)], feature_group_count=w.shape[0], dimension_numbers=('NCH', 'OIH', 'NCH'))
            y = y + b[None, :, None]
            return jnp.transpose(y, (0, 2, 1))

        def selective_scan(u, delta, A, Bm, Cm, D):

            def step(h, inp):
                u_t, d_t, B_t, C_t = inp
                dA = jnp.exp(d_t[..., None] * A)
                h = dA * h + (d_t * u_t)[..., None] * B_t[:, None, :]
                y = jnp.einsum('bdn,bn->bd', h, C_t)
                return (h, y)
            h0 = jnp.zeros((u.shape[0], A.shape[0], A.shape[1]), u.dtype)
            xs = (jnp.transpose(u, (1, 0, 2)), jnp.transpose(delta, (1, 0, 2)), jnp.transpose(Bm, (1, 0, 2)), jnp.transpose(Cm, (1, 0, 2)))
            _, ys = lax.scan(step, h0, xs)
            return jnp.transpose(ys, (1, 0, 2)) + u * D

        def mamba(seq, p):
            in_w, conv_w, conv_b, xp_w, dt_w, dt_b, A_log, Dp, out_w = p
            di = in_w.shape[0] // 2
            xz = jnp.einsum('blc,ec->ble', seq, in_w)
            x, z = (xz[..., :di], xz[..., di:])
            x = silu(causal_conv(x, conv_w, conv_b))
            xdbl = jnp.einsum('bld,ed->ble', x, xp_w)
            dtr = dt_w.shape[1]
            dt = xdbl[..., :dtr]
            Bm = xdbl[..., dtr:dtr + D_STATE]
            Cm = xdbl[..., dtr + D_STATE:]
            delta = jax.nn.softplus(jnp.einsum('blr,dr->bld', dt, dt_w) + dt_b)
            A = -jnp.exp(A_log)
            y = selective_scan(x, delta, A, Bm, Cm, Dp)
            y = y * silu(z)
            return jnp.einsum('bld,cd->blc', y, out_w)

        def run_bidir(seq, p):
            f = mamba(seq, p)
            r = jnp.flip(mamba(jnp.flip(seq, 1), p), 1)
            return 0.5 * (f + r)

        def _mamba_params(key, c):
            di = 2 * c
            dtr = max(1, -(-c // 16))
            ks = jax.random.split(key, 7)
            in_w = jax.random.normal(ks[0], (2 * di, c), jnp.float32) * 0.02
            conv_w = jax.random.normal(ks[1], (di, 1, D_CONV), jnp.float32) * 0.1
            conv_b = jnp.zeros((di,), jnp.float32)
            xp_w = jax.random.normal(ks[2], (dtr + 2 * D_STATE, di), jnp.float32) * 0.02
            dt_w = jax.random.normal(ks[3], (di, dtr), jnp.float32) * 0.1
            dt_b = jax.random.normal(ks[4], (di,), jnp.float32) * 0.1 - 4.0
            A_log = jnp.log(jnp.broadcast_to(jnp.arange(1.0, D_STATE + 1.0, dtype=jnp.float32), (di, D_STATE)))
            Dp = jnp.ones((di,), jnp.float32)
            out_w = jax.random.normal(ks[5], (c, di), jnp.float32) * 0.02
            return (in_w, conv_w, conv_b, xp_w, dt_w, dt_b, A_log, Dp, out_w)
        rp = (row_in_w, row_conv_w, row_conv_b, row_xp_w, row_dt_w, row_dt_b, row_A_log, row_D, row_out_w)
        cp = (col_in_w, col_conv_w, col_conv_b, col_xp_w, col_dt_w, col_dt_b, col_A_log, col_D, col_out_w)
        b, c, h, w = x.shape
        xr = jnp.transpose(x, (0, 2, 3, 1)).reshape(b * h, w, c)
        xr = run_bidir(xr, rp).reshape(b, h, w, c)
        xr = jnp.transpose(xr, (0, 3, 1, 2))
        xc = jnp.transpose(x, (0, 3, 2, 1)).reshape(b * w, h, c)
        xc = run_bidir(xc, cp).reshape(b, w, h, c)
        xc = jnp.transpose(xc, (0, 3, 2, 1))
        x_rec = 0.5 * (xr + xc)
        g = 4
        xg = x_rec.reshape(b, g, c // g, h, w)
        mu = jnp.mean(xg, axis=(2, 3, 4), keepdims=True)
        var = jnp.var(xg, axis=(2, 3, 4), keepdims=True)
        xg = (xg - mu) * lax.rsqrt(var + GN_EPS)
        xn = xg.reshape(b, c, h, w) * gn_w[None, :, None, None] + gn_b[None, :, None, None]
        return silu(xn) + x

    def _L1_conv_ref(x, origin_weight, P_weight, new_param, bn1_gamma, bn1_beta, bn2_gamma, bn2_beta):
        import jax, jax.numpy as jnp
        import numpy as np
        from jax import lax
        KSHAPE = (64, 64, 3, 3)
        KSIZE = 64 * 64 * 9
        EPS = 1e-05

        def _conv3x3(x, w, stride):
            return lax.conv_general_dilated(x, w, window_strides=(stride, stride), padding=[(1, 1), (1, 1)], dimension_numbers=('NCHW', 'OIHW', 'NCHW'))

        def _batchnorm(x, gamma, beta):
            mean = jnp.mean(x, axis=(0, 2, 3), keepdims=True)
            var = jnp.var(x, axis=(0, 2, 3), keepdims=True)
            xhat = (x - mean) * lax.rsqrt(var + EPS)
            return xhat * gamma[None, :, None, None] + beta[None, :, None, None]
        w1 = (origin_weight[0:KSIZE] + jnp.einsum('i,if->f', new_param, P_weight[:, 0:KSIZE])).reshape(KSHAPE)
        out = _conv3x3(x, w1, stride=1)
        out = jax.nn.relu(_batchnorm(out, bn1_gamma, bn1_beta))
        w2 = (new_param[39] * origin_weight[KSIZE:2 * KSIZE] + jnp.einsum('i,if->f', new_param, P_weight[:, KSIZE:2 * KSIZE])).reshape(KSHAPE)
        out2 = _batchnorm(_conv3x3(out, w2, stride=1), bn2_gamma, bn2_beta)
        out2 = out2 + x
        return jax.nn.relu(out2)

    def _gn(v, G=32, eps=1e-5):
        B_, C_, H_, W_ = v.shape
        g = v.reshape(B_, G, C_ // G, H_, W_)
        m = jnp.mean(g, axis=(2, 3, 4), keepdims=True)
        s = jnp.var(g, axis=(2, 3, 4), keepdims=True)
        return ((g - m) / jnp.sqrt(s + eps)).reshape(v.shape)

    def _ln_c(v, eps=1e-6):
        m = jnp.mean(v, axis=1, keepdims=True)
        s = jnp.var(v, axis=1, keepdims=True)
        return (v - m) / jnp.sqrt(s + eps)

    def _ln_t(v, eps=1e-5):
        m = jnp.mean(v, axis=-1, keepdims=True)
        s = jnp.var(v, axis=-1, keepdims=True)
        return (v - m) / jnp.sqrt(s + eps)

    def _to_tokens(v):
        B_, C_, H_, W_ = v.shape
        return v.reshape(B_, C_, H_ * W_).transpose(0, 2, 1)
    def _from_tokens(t, like):
        B_, C_, H_, W_ = like.shape
        return t.transpose(0, 2, 1).reshape(B_, C_, H_, W_)

    x = _L0_conv_ref(x, L0_conv_row_in_w, L0_conv_row_conv_w, L0_conv_row_conv_b, L0_conv_row_xp_w, L0_conv_row_dt_w, L0_conv_row_dt_b, L0_conv_row_A_log, L0_conv_row_D, L0_conv_row_out_w, L0_conv_col_in_w, L0_conv_col_conv_w, L0_conv_col_conv_b, L0_conv_col_xp_w, L0_conv_col_dt_w, L0_conv_col_dt_b, L0_conv_col_A_log, L0_conv_col_D, L0_conv_col_out_w, L0_conv_gn_w, L0_conv_gn_b)
    x = _L1_conv_ref(x, L1_conv_origin_weight, L1_conv_P_weight, L1_conv_new_param, L1_conv_bn1_gamma, L1_conv_bn1_beta, L1_conv_bn2_gamma, L1_conv_bn2_beta)
    return x


_drawn_inputs = setup_inputs


def setup_inputs(seed=0):
    import zlib

    import numpy as np

    out = dict(_drawn_inputs(seed))
    spreads = {'L0_conv_row_conv_b': (0.0, 0.1),
     'L0_conv_row_D': (1.0, 0.6),
     'L0_conv_col_conv_b': (0.0, 0.1),
     'L0_conv_col_D': (1.0, 0.6),
     'L0_conv_gn_w': (1.0, 0.6),
     'L0_conv_gn_b': (0.0, 0.1),
     'L1_conv_bn1_gamma': (1.0, 0.2),
     'L1_conv_bn1_beta': (0.0, 0.1),
     'L1_conv_bn2_gamma': (1.0, 0.2),
     'L1_conv_bn2_beta': (0.0, 0.1)}
    factors = {'L0_conv_row_conv_w': 2.729,
     'L0_conv_row_xp_w': 8.0,
     'L0_conv_row_dt_w': 8.0,
     'L0_conv_row_dt_b': 8.0,
     'L0_conv_row_A_log': 8.0,
     'L0_conv_col_xp_w': 8.0,
     'L0_conv_col_dt_w': 8.0,
     'L0_conv_col_dt_b': 8.0,
     'L0_conv_col_A_log': 8.0}
    for name, (base, spread) in spreads.items():
        noise = np.random.default_rng([zlib.crc32(name.encode()), seed]).standard_normal(out[name].shape)
        drawn = base * np.exp(spread * noise) if base else spread * noise
        out[name] = jnp.asarray(drawn.astype(out[name].dtype))
    for name, factor in factors.items():
        out[name] = (out[name] * factor).astype(out[name].dtype)
    return out
```

```python
from contextlib import ExitStack

import concourse.bass as bass
from concourse import mybir

F32 = mybir.dt.float32
BF16 = mybir.dt.bfloat16
ALU = mybir.AluOpType
ACT = mybir.ActivationFunctionType

P = 128
BATCH, CH, SIDE = 8, 64, 128
DI, NS, DTR, TAPS = 128, 16, 4, 4
SEQS = 8
PX = SEQS * SIDE
HALF = 512
PAD = SIDE + 2 * (TAPS - 1)
TILES = BATCH * SIDE // SEQS
GROUPS = DI // 8
UNIT = 2 * GROUPS
SLOTS = 2 * UNIT
YB = SLOTS // 4
STEPS = 20
LEAD = 7
STACK_DMAS = 24
FWD, REV = 0, 1
B_RING, H_RING, C_RING = 4, 4, 8
GN_GROUPS, EPS = 4, 1e-5
KEYS = 40
KTAPS = 9
KSIZE = CH * CH * KTAPS


def at_least(engine, semaphore, value):
    if isinstance(value, int) and value <= 0:
        return
    engine.wait_ge(semaphore, value)


def group_of(slot):
    d, q = divmod(slot, UNIT)
    half, r = divmod(q, GROUPS)
    k, j = divmod(r, 4)
    return d, half, k, j


def delta_bank_before(slot):
    q = slot % UNIT
    if q >= 3:
        return 3
    return {0: 2, 1: 2, 2: 5}[q]


def scan_stage(nc, xs, rec, weights, consts):
    with ExitStack() as ctx:
        def sb(name, shape, dt=F32):
            return ctx.enter_context(nc.sbuf_tensor(name, shape, dt))

        def pb(name, shape):
            return ctx.enter_context(nc.psum_tensor(name, shape, F32))

        def sem(name):
            return ctx.enter_context(nc.semaphore(name))

        in_t = [sb(f"in_t{s}", [P, 2 * DI]) for s in range(2)]
        taps = [sb(f"taps{s}", [P, 4, DI]) for s in range(2)]
        conv_in = taps
        xp_t = [sb(f"xp_t{s}", [P, DTR + 2 * NS]) for s in range(2)]
        xp_dt = [sb(f"xp_dt{s}", [DTR, DI]) for s in range(2)]
        dt_t = [sb(f"dt_t{s}", [DTR, DI]) for s in range(2)]
        to_b = [sb(f"to_b{s}", [P, P]) for s in range(2)]
        to_c = [sb(f"to_c{s}", [P, P]) for s in range(2)]
        to_dt = [sb(f"to_dt{s}", [P, P]) for s in range(2)]
        out_t = [sb(f"out_t{s}", [P, CH]) for s in range(2)]
        a_neg = [sb(f"a_neg{s}", [P, GROUPS]) for s in range(2)]
        cols = [sb(f"cols{s}", [P, 3]) for s in range(2)]
        sel_f = sb("sel_f", [P, 4 * P + 4 * 32])
        spread = sb("spread", [P, 4, P], BF16)
        gather = sel_f[:, 4 * P:].rearrange("p (k m) -> p k m", k=4)

        xt = sb("xt", [P, SEQS, PAD])
        u = [sb(f"u{d}", [P, PX]) for d in range(2)]
        zs = sb("zs", [P, PX])
        b_rep = [sb(f"b_rep{d}", [P, PX]) for d in range(2)]
        c_rep = [sb(f"c_rep{d}", [P, PX]) for d in range(2)]
        expabs = sb("expabs", [P, PX])
        onep = sb("onep", [P, PX])
        lnp = sb("lnp", [P, PX])
        vpos = sb("vpos", [P, PX])
        delta = sb("delta", [P, PX])
        du = sb("du", [P, PX])
        d_parts = [sb(f"d_parts{d}", [P, 3, PX], BF16) for d in range(2)]
        u_parts = sb("u_parts", [P, 3, PX], BF16)
        d_stack = [sb(f"d_stack{d}", [96, 4, PX], BF16) for d in range(2)]
        u_stack = [sb(f"u_stack{d}", [96, 4, PX], BF16) for d in range(2)]
        drive = sb("drive", [P, B_RING, HALF])
        state = sb("state", [P, H_RING, HALF])
        read = sb("read", [P, C_RING, HALF])
        y_fwd = sb("y_fwd", [P, PX])
        y_sum = sb("y_sum", [P, HALF])
        gated = sb("gated", [P, 2, HALF])
        o_sb = sb("o_sb", [CH, 2, HALF])

        d_bank = [pb(f"d_bank{n}", [P, HALF]) for n in range(3)]
        u_bank = [pb(f"u_bank{n}", [P, HALF]) for n in range(2)]
        y_bank = pb("y_bank", [P, HALF])
        p_bank = [pb(f"p_bank{n}", [P, HALF]) for n in range(2)]

        s_load = sem("weights_loaded")
        s_prep = sem("weights_prepared")
        s_dtw = sem("dt_weights_multiplied")
        s_exp_a = sem("a_exponentiated")
        s_x = sem("x_loaded")
        s_delta_b = sem("delta_spread")
        s_du_b = sem("du_spread")
        s_decay = sem("decay_ready")
        s_drive = sem("drive_ready")
        s_state = sem("state_ready")
        s_read = sem("read_ready")
        s_ysum = sem("y_batch_summed")
        s_yout = sem("y_taken")
        s_gate = sem("gated_ready")
        s_proj = sem("projection_ready")
        s_evac = sem("projection_taken")
        s_soft = sem("softplus_parts")
        s_delta = sem("delta_steps")
        s_hi = sem("high_parts")
        s_rest = sem("rests")
        s_mid = sem("middle_parts")
        s_low = sem("low_parts")
        s_stack = sem("stacked")
        s_store = sem("rec_stored")
        s_half = sem("reverse_parts_added")

        n_load = 0

        def seqs(ap):
            return ap.rearrange("p (s t) -> p s t", t=SIDE)

        def inner(ap, d):
            v = seqs(ap)
            return v[:, :, 1:SIDE] if d == FWD else v[:, :, 0:SIDE - 1]

        def first(ap, d):
            v = seqs(ap)
            return v[:, :, 0:1] if d == FWD else v[:, :, SIDE - 1:SIDE]

        def px(h):
            return slice(h * HALF, (h + 1) * HALF)

        block = ctx.enter_context(nc.Block())

        def wset(i):
            return 0 if i < TILES else 1

        def over_tiles(engine, body, tail):
            body(0, 0, None, 0)
            with engine.Fori(1, TILES - 1) as i:
                body(i, 0, 0, 0)
            body(TILES - 1, 0, 0, 1)
            body(TILES, 1, 0, 1)
            with engine.Fori(TILES + 1, 2 * TILES - 1) as i:
                body(i, 1, 1, 1)
            body(2 * TILES - 1, 1, 1, None)
            tail(2 * TILES)

        def plan(base, s0):
            kinds = [("b", 0), ("b", 1), ("c", 0), ("c", 1), ("dt", 0), ("dt", 1)]
            return [(base + 9 + n, s0 + n, kind, h) for n, (kind, h) in enumerate(kinds)]

        REV_PLAN = plan(0, 5)
        FWD_PLAN = plan(UNIT, 13)

        @block.sync
        def _(sp):
            def load(dst, src):
                sp.dma_start(dst, src).then_inc(s_load, 16)

            for s in range(2):
                w = weights[s]
                for half in range(2):
                    load(in_t[s][64 * half:64 * half + 64, :], w["in_t"])
                for m, pair in enumerate(((3, 2), (1, 0), (2, 3), (0, 1))):
                    for half in range(2):
                        row = w["conv_t"][pair[half]:pair[half] + 1, :]
                        load(taps[s][64 * half:64 * half + 64, m, :],
                             bass.AP(row.tensor, row.offset, [[0, 64], [1, DI]]))
                load(xp_t[s][:, :], w["xp_t"])
                load(xp_dt[s][:, :], w["xp_dt"])
                load(dt_t[s][:, :], w["dt_t"])
                load(out_t[s][:, :], w["out_t"])
                load(a_neg[s][:, :], w["a_log"])
                load(cols[s][:, :], w["cols"])
            load(sel_f[:, :], consts)

            def load_x(tile):
                x = xs[bass.ds(tile, 1)].rearrange("n c (s t) -> (n c) s t", t=SIDE)
                sp.dma_start(xt[0:64, :, 3:3 + SIDE], x).then_inc(s_x, 16)
                sp.dma_start(xt[64:128, :, 4:4 + SIDE], x).then_inc(s_x, 16)

            def stack(unit, d, free_at):
                at_least(sp, s_du_b, free_at)
                at_least(sp, s_delta_b, free_at)
                for part, ready in ((0, s_hi), (1, s_mid), (2, s_low)):
                    for t, (parts, stacked) in enumerate(((d_parts[d], d_stack[d]),
                                                          (u_parts, u_stack[d]))):
                        sp.wait_ge(ready, unit * 2 + t + 1)
                        for j in range(4):
                            sp.dma_start(stacked[32 * part:32 * part + 32, j, :],
                                         parts[32 * j:32 * j + 32, part, :]).then_inc(s_stack, 16)

            def store(tile, half, count):
                sp.wait_ge(s_evac, count)
                dst = rec[bass.ds(tile, 1)].rearrange("n c p -> (n c) p")
                sp.dma_start(dst[:, px(half)], o_sb[:, half, :]).then_inc(s_store, 16)

            sp.wait_ge(s_prep, 1)
            load_x(0)
            stack(0, FWD, 0)

            def body(i, cur, prev, nxt):
                base = LEAD + STEPS * i
                rev_free, fwd_free = SLOTS * i, SLOTS * i + UNIT
                if prev is not None:
                    store(i - 1, 1, base + 1)
                if nxt is not None:
                    sp.wait_ge(s_proj, base + 5)
                    load_x(i + 1)
                stack(2 * i + 1, REV, rev_free)
                if nxt is not None:
                    stack(2 * i + 2, FWD, fwd_free)
                store(i, 0, base + (STEPS if nxt is not None else STEPS - 8))

            def tail(i):
                store(i - 1, 1, LEAD + STEPS * i - 8 + 1)
                sp.wait_ge(s_store, 16 * 2 * i)

            over_tiles(sp, body, tail)

        N_LOAD = 16 * (2 * 16 + 1)

        @block.tensor
        def _(pe):
            pe.wait_ge(s_load, N_LOAD)
            for s in range(2):
                nc.tensor.matmul(p_bank[s][:, 0:P], xp_dt[s][:, :], dt_t[s][:, :],
                                 start=True, stop=True).then_inc(s_dtw, 1)

            def begin(step):
                at_least(pe, s_evac, step - 1)

            def project(step, lhs, rhs, rows, bank):
                nc.tensor.matmul(p_bank[bank][0:rows, :], lhs, rhs, start=True,
                                 stop=True).then_inc(s_proj, 1)

            def conv_step(step, bank, s, d, h):
                begin(step)
                rows = slice(4 * h, 4 * h + 4)
                offs = (3, 1) if d == FWD else (4, 6)
                nc.tensor.matmul(p_bank[bank][:, :], conv_in[s][:, 2 * d, :],
                                 xt[:, rows, offs[0]:offs[0] + SIDE], start=True, stop=False)
                nc.tensor.matmul(p_bank[bank][:, :], conv_in[s][:, 2 * d + 1, :],
                                 xt[:, rows, offs[1]:offs[1] + SIDE], start=False,
                                 stop=True).then_inc(s_proj, 1)

            def z_step(step, bank, s, h):
                begin(step)
                project(step, in_t[s][0:64, DI:2 * DI], xt[0:64, 4 * h:4 * h + 4, 3:3 + SIDE], P, bank)

            def bcd_step(step, bank, s, d, kind, h, u_ready):
                begin(step)
                pe.wait_ge(s_evac, u_ready)
                lhs = {"b": to_b, "c": to_c, "dt": to_dt}[kind][s]
                project(step, lhs[:, :], u[d][:, px(h)], P, bank)

            def out_step(step, bank, s, half, tile):
                begin(step)
                pe.wait_ge(s_gate, 2 * tile + half + 1)
                project(step, out_t[s][:, :], gated[:, half, :], CH, bank)

            def spread_group(i, slot):
                d, half, k, j = group_of(slot)
                g = SLOTS * i + slot
                if slot % UNIT == 0:
                    pe.wait_ge(s_stack, 16 * STACK_DMAS * (2 * i + d + 1))
                at_least(pe, s_state, g - delta_bank_before(slot) + 1)
                nc.tensor.matmul(d_bank[slot % UNIT % 3][:, :], spread[0:96, k, :],
                                 d_stack[d][:, j, px(half)], start=True,
                                 stop=True).then_inc(s_delta_b, 1)
                at_least(pe, s_drive, g - 1)
                nc.tensor.matmul(u_bank[slot % 2][:, :], spread[0:96, k, :],
                                 u_stack[d][:, j, px(half)], start=True,
                                 stop=True).then_inc(s_du_b, 1)

            def sum_batch(i, b):
                k = b % 4
                pe.wait_ge(s_read, SLOTS * i + 4 * b + 4)
                if k == 0:
                    at_least(pe, s_yout, 4 * i + b // 4)
                for j in range(4):
                    mm = nc.tensor.matmul(y_bank[32 * j:32 * j + 32, :], gather[:, k, :],
                                          read[:, (4 * b + j) % C_RING, :],
                                          start=(k == 0), stop=(k == 3),
                                          tile_position=(0, 32 * j))
                mm.then_inc(s_ysum, 1)

            pe.wait_ge(s_prep, 4)
            pe.wait_ge(s_x, 32)
            for n in range(8):
                bank = (n + 1) % 2
                if n < 2:
                    conv_step(n, bank, 0, FWD, n)
                else:
                    kind = ("b", "c", "dt")[(n - 2) // 2]
                    bcd_step(n, bank, 0, FWD, kind, n % 2, 2)

            def body(i, cur, prev, nxt):
                base = LEAD + STEPS * i
                steps = {}
                if prev is not None:
                    steps.setdefault(7, []).append(lambda: out_step(base, 0, prev, 1, i - 1))
                steps.setdefault(7, []).append(lambda: conv_step(base + 1, 1, cur, REV, 0))
                steps.setdefault(7, []).append(lambda: conv_step(base + 2, 0, cur, REV, 1))
                steps[8] = [lambda: z_step(base + 3, 1, cur, 0), lambda: z_step(base + 4, 0, cur, 1)]
                for slot, step, kind, h in REV_PLAN:
                    steps[slot] = [lambda a=(base + step, step % 2, cur, REV, kind, h, base + 3):
                                   bcd_step(*a)]
                if nxt is not None:
                    def x_steps():
                        pe.wait_ge(s_x, 32 * (i + 2))
                        conv_step(base + 11, 1, nxt, FWD, 0)
                        conv_step(base + 12, 0, nxt, FWD, 1)
                    steps[UNIT + 7] = [x_steps]
                    for slot, step, kind, h in FWD_PLAN:
                        steps[slot] = [lambda a=(base + step, step % 2, nxt, FWD, kind, h, base + 13):
                                       bcd_step(*a)]
                last = base + (19 if nxt is not None else 11)
                steps[56] = [lambda: out_step(last, 1, cur, 0, i)]
                for slot in range(SLOTS):
                    spread_group(i, slot)
                    for f in steps.get(slot, []):
                        f()
                    if slot % 4 == 0:
                        b = slot // 4 - 2
                        if b >= 0:
                            sum_batch(i, b)
                        elif prev is not None:
                            sum_batch(i - 1, b + YB)

            def tail(i):
                sum_batch(i - 1, YB - 2)
                sum_batch(i - 1, YB - 1)
                out_step(LEAD + STEPS * i - 8, 0, 1, 1, i - 1)

            over_tiles(pe, body, tail)

        @block.scalar
        def _(act):
            act.wait_ge(s_load, N_LOAD)
            for s in range(2):
                nc.scalar.activation(a_neg[s][:, :], a_neg[s][:, :], ACT.Exp).then_inc(s_exp_a, 1)

            def take_silu(count, bank, out, bias):
                act.wait_ge(s_proj, count)
                nc.scalar.activation(out, p_bank[bank][:, :], ACT.Silu,
                                     **({"bias": bias} if bias is not None else {})).then_inc(s_evac, 1)

            def take(count, bank, s, d, kind, h, used):
                act.wait_ge(s_proj, count)
                src = p_bank[bank][:, :]
                if kind == "b":
                    at_least(act, s_drive, used)
                    nc.scalar.copy(b_rep[d][:, px(h)], src).then_inc(s_evac, 1)
                elif kind == "c":
                    at_least(act, s_read, used)
                    nc.scalar.copy(c_rep[d][:, px(h)], src).then_inc(s_evac, 1)
                else:
                    nc.scalar.activation(expabs[:, px(h)], src, ACT.Abs, bias=cols[s][:, 1:2])
                    nc.scalar.activation(vpos[:, px(h)], src, ACT.Relu,
                                         bias=cols[s][:, 1:2]).then_inc(s_evac, 1)

            def take_out(count, bank, half, tile):
                act.wait_ge(s_proj, count)
                at_least(act, s_store, 16 * (2 * tile + half - 1))
                nc.scalar.copy(o_sb[:, half, :], p_bank[bank][0:CH, :]).then_inc(s_evac, 1)

            def softplus(unit, evac):
                act.wait_ge(s_evac, evac)
                nc.scalar.activation(expabs[:, :], expabs[:, :], ACT.Exp, scale=-1.0).then_inc(s_soft, 1)
                act.wait_ge(s_soft, 3 * unit + 1)
                nc.scalar.activation(onep[:, :], expabs[:, :], ACT.Identity, bias=1.0).then_inc(s_soft, 1)
                nc.scalar.activation(lnp[:, :], expabs[:, :], ACT.Ln, bias=1.0).then_inc(s_soft, 1)

            def high(unit, d, t):
                act.wait_ge(s_delta, 4 * unit + 3 + t)
                at_least(act, s_stack, 16 * STACK_DMAS * unit)
                if t == 0:
                    nc.scalar.copy(inner(d_parts[d][:, 0, :], d), inner(delta[:, :], d)).then_inc(s_hi, 1)
                else:
                    nc.scalar.copy(u_parts[:, 0, :], du[:, :]).then_inc(s_hi, 1)

            def middle(unit, d, t):
                act.wait_ge(s_rest, 2 * unit + 1 + t)
                if t == 0:
                    nc.scalar.copy(inner(d_parts[d][:, 1, :], d), inner(delta[:, :], d)).then_inc(s_mid, 1)
                else:
                    nc.scalar.copy(u_parts[:, 1, :], du[:, :]).then_inc(s_mid, 1)

            act.wait_ge(s_prep, 4)
            for n in range(8):
                bank = (n + 1) % 2
                if n < 2:
                    take_silu(n + 1, bank, u[FWD][:, px(n)], cols[0][:, 0:1])
                else:
                    take(n + 1, bank, 0, FWD, ("b", "c", "dt")[(n - 2) // 2], n % 2, 0)
            softplus(0, 8)
            for f in (high, middle):
                for t in range(2):
                    f(0, FWD, t)

            def body(i, cur, prev, nxt):
                base = LEAD + STEPS * i
                steps = {n: [] for n in range(SLOTS)}
                if prev is not None:
                    steps[7].append(lambda: take_out(base + 1, 0, 1, i - 1))

                def silu_rev():
                    at_least(act, s_yout, 4 * i)
                    take_silu(base + 2, 1, u[REV][:, px(0)], cols[cur][:, 0:1])
                    take_silu(base + 3, 0, u[REV][:, px(1)], cols[cur][:, 0:1])
                    at_least(act, s_gate, 2 * i)
                    take_silu(base + 4, 1, zs[:, px(0)], None)
                    take_silu(base + 5, 0, zs[:, px(1)], None)
                steps[8].append(silu_rev)
                for slot, step, kind, h in REV_PLAN:
                    steps[slot + 1].append(lambda a=(base + step + 1, step % 2, cur, REV, kind, h,
                                                     SLOTS * i): take(*a))
                units = [(0, 2 * i + 1, REV, base + 11)]
                if nxt is not None:
                    def silu_fwd():
                        act.wait_ge(s_yout, 4 * i + 2)
                        take_silu(base + 12, 1, u[FWD][:, px(0)], cols[nxt][:, 0:1])
                        take_silu(base + 13, 0, u[FWD][:, px(1)], cols[nxt][:, 0:1])
                    steps[UNIT + 8].append(silu_fwd)
                    for slot, step, kind, h in FWD_PLAN:
                        steps[slot + 1].append(lambda a=(base + step + 1, step % 2, nxt, FWD, kind, h,
                                                         SLOTS * i + UNIT): take(*a))
                    units.append((UNIT, 2 * i + 2, FWD, base + 19))
                for at, unit, d, evac in units:
                    steps[at + 16].append(lambda a=(unit, evac): softplus(*a))
                    steps[at + 21].append(lambda a=(unit, d, 0): high(*a))
                    steps[at + 22].append(lambda a=(unit, d, 1): high(*a))
                    steps[at + 25].append(lambda a=(unit, d, 0): middle(*a))
                    steps[at + 26].append(lambda a=(unit, d, 1): middle(*a))
                last = base + (19 if nxt is not None else 11)
                steps[57].append(lambda: take_out(last + 1, 1, 0, i))
                for slot in range(SLOTS):
                    d, half, k, j = group_of(slot)
                    bank = d_bank[slot % UNIT % 3]
                    act.wait_ge(s_delta_b, SLOTS * i + slot + 1)
                    nc.scalar.activation(inner(bank[:, :], d), inner(bank[:, :], d), ACT.Exp,
                                         scale=a_neg[cur][:, 4 * j + k:4 * j + k + 1]).then_inc(s_decay, 1)
                    for f in steps[slot]:
                        f()

            def tail(i):
                take_out(LEAD + STEPS * i - 8 + 1, 0, 1, i - 1)

            over_tiles(act, body, tail)

        @block.vector
        def _(dve):
            nc.vector.memset(xt[:, :, :], 0.0).then_inc(s_prep, 1)
            for d in range(2):
                for part in range(3):
                    ins = nc.vector.memset(first(d_parts[d][:, part, :], d), 0.0)
            ins.then_inc(s_prep, 1)
            dve.wait_ge(s_load, N_LOAD)
            nc.vector.tensor_copy(spread[0:96, :, :],
                                  sel_f[0:96, 0:4 * P].rearrange("p (k m) -> p k m", k=4))
            for s in range(2):
                tap = taps[s]
                w = in_t[s][:, 0:DI]
                nc.vector.tensor_tensor(tap[:, :, :], tap[:, :, :],
                                        w.unsqueeze(1).broadcast_to([P, 4, DI]), ALU.mult)
                for dst, c0 in ((to_b[s], DTR), (to_c[s], DTR + NS)):
                    nc.vector.tensor_copy(dst[:, :].rearrange("p (n r) -> p n r", r=8),
                                          xp_t[s][:, c0:c0 + NS].unsqueeze(2).broadcast_to([P, NS, 8]))
                dve.wait_ge(s_dtw, s + 1)
                nc.vector.tensor_copy(to_dt[s][:, :], p_bank[s][:, 0:P])
                dve.wait_ge(s_exp_a, s + 1)
                nc.vector.tensor_scalar(a_neg[s][:, :], a_neg[s][:, :], -1.0, None,
                                        ALU.mult).then_inc(s_prep, 1)

            def finish_delta(unit):
                dve.wait_ge(s_soft, 3 * unit + 3)
                at_least(dve, s_mid, 2 * unit)
                at_least(dve, s_low, 2 * unit)
                nc.vector.scalar_tensor_tensor(out=delta[:, :], in0=onep[:, :], scalar=-1.0,
                                               in1=expabs[:, :], op0=ALU.add,
                                               op1=ALU.subtract).then_inc(s_delta, 1)
                dve.wait_ge(s_delta, 4 * unit + 1)
                nc.vector.tensor_tensor(delta[:, :], lnp[:, :], delta[:, :],
                                        ALU.subtract).then_inc(s_delta, 1)

            def finish_du(unit, d):
                dve.wait_ge(s_delta, 4 * unit + 2)
                nc.vector.tensor_tensor(delta[:, :], delta[:, :], vpos[:, :],
                                        ALU.add).then_inc(s_delta, 1)
                dve.wait_ge(s_delta, 4 * unit + 3)
                nc.vector.tensor_tensor(du[:, :], delta[:, :], u[d][:, :], ALU.mult).then_inc(s_delta, 1)

            def rest(unit, d, t):
                dve.wait_ge(s_hi, 2 * unit + 1 + t)
                dve.wait_ge(s_delta, 4 * unit + 4)
                src = (delta, du)[t]
                if t == 0:
                    src, hi = inner(delta[:, :], d), inner(d_parts[d][:, 0, :], d)
                else:
                    src, hi = du[:, :], u_parts[:, 0, :]
                nc.vector.tensor_tensor(src, src, hi, ALU.subtract).then_inc(s_rest, 1)

            def make_drive(i, slot):
                d, half, k, j = group_of(slot)
                g = SLOTS * i + slot
                dve.wait_ge(s_du_b, g + 1)
                at_least(dve, s_state, g - B_RING + 1)
                nc.vector.tensor_tensor(drive[:, slot % B_RING, :], u_bank[slot % 2][:, :],
                                        b_rep[d][:, px(half)], ALU.mult).then_inc(s_drive, 1)

            def scan(i, slot):
                d, half, k, j = group_of(slot)
                g = SLOTS * i + slot
                dve.wait_ge(s_decay, g + 1)
                dve.wait_ge(s_drive, g + 1)
                at_least(dve, s_read, g - H_RING + 1)
                step = 1 if d == FWD else -1
                nc.vector.tensor_tensor_scan(state[:, slot % H_RING, ::step],
                                             d_bank[slot % UNIT % 3][:, ::step],
                                             drive[:, slot % B_RING, ::step], 0.0,
                                             ALU.mult, ALU.add).then_inc(s_state, 1)

            def take_y(i, e, s):
                d, half = divmod(e, 2)
                dve.wait_ge(s_ysum, YB * i + 4 * e + 4)
                out = y_fwd[:, px(half)] if d == FWD else y_sum[:, :]
                if d == REV:
                    at_least(dve, s_gate, 2 * i + half)
                else:
                    at_least(dve, s_half, 2 * i + half - 1)
                nc.vector.scalar_tensor_tensor(out=out, in0=u[d][:, px(half)], scalar=cols[s][:, 2:3],
                                               in1=y_bank[:, :], op0=ALU.mult,
                                               op1=ALU.add).then_inc(s_yout, 1)
                if d == REV:
                    dve.wait_ge(s_yout, 4 * i + e + 1)
                    nc.vector.tensor_tensor(y_sum[:, :], y_sum[:, :], y_fwd[:, px(half)],
                                            ALU.add).then_inc(s_half, 1)
                    dve.wait_ge(s_half, 2 * i + half + 1)
                    at_least(dve, s_evac, LEAD + STEPS * i + (0 if half == 0 else 1) - 0)
                    nc.vector.tensor_tensor(gated[:, half, :], y_sum[:, :], zs[:, px(half)],
                                            ALU.mult).then_inc(s_gate, 1)

            finish_delta(0)
            finish_du(0, FWD)
            for t in range(2):
                rest(0, FWD, t)

            def body(i, cur, prev, nxt):
                steps = {n: [] for n in range(SLOTS)}
                if prev is not None:
                    steps[5].append(lambda: take_y(i - 1, 3, prev))
                for e in range(3):
                    steps[16 * e + 21].append(lambda e=e: take_y(i, e, cur))
                units = [(0, 2 * i + 1, REV)] + ([(UNIT, 2 * i + 2, FWD)] if nxt is not None else [])
                for at, unit, d in units:
                    steps[at + 17].append(lambda a=unit: finish_delta(a))
                    steps[at + 18].append(lambda a=(unit, d): finish_du(*a))
                    steps[at + 22].append(lambda a=(unit, d, 0): rest(*a))
                    steps[at + 23].append(lambda a=(unit, d, 1): rest(*a))
                for slot in range(SLOTS):
                    make_drive(i, slot)
                    if slot > 0:
                        scan(i, slot - 1)
                    elif prev is not None:
                        scan(i - 1, SLOTS - 1)
                    for f in steps[slot]:
                        f()

            def tail(i):
                scan(i - 1, SLOTS - 1)
                take_y(i - 1, 3, 1)

            over_tiles(dve, body, tail)

        @block.gpsimd
        def _(pool):
            def low(unit, d, t):
                pool.wait_ge(s_mid, 2 * unit + 1 + t)
                if t == 0:
                    nc.gpsimd.tensor_tensor(inner(d_parts[d][:, 2, :], d), inner(delta[:, :], d),
                                            inner(d_parts[d][:, 1, :], d), ALU.subtract).then_inc(s_low, 1)
                else:
                    nc.gpsimd.tensor_tensor(u_parts[:, 2, :], du[:, :], u_parts[:, 1, :],
                                            ALU.subtract).then_inc(s_low, 1)

            for t in range(2):
                low(0, FWD, t)

            def body(i, cur, prev, nxt):
                steps = {n: [] for n in range(SLOTS)}
                units = [(0, 2 * i + 1, REV)] + ([(UNIT, 2 * i + 2, FWD)] if nxt is not None else [])
                for at, unit, d in units:
                    steps[at + 24].append(lambda a=(unit, d, 0): low(*a))
                    steps[at + 25].append(lambda a=(unit, d, 1): low(*a))
                for slot in range(SLOTS):
                    d, half, k, j = group_of(slot)
                    pool.wait_ge(s_state, SLOTS * i + slot + 1)
                    at_least(pool, s_ysum, YB * i + slot // 4 - C_RING // 4 + 1)
                    nc.gpsimd.tensor_tensor(read[:, slot % C_RING, :], state[:, slot % H_RING, :],
                                            c_rep[d][:, px(half)], ALU.mult).then_inc(s_read, 1)
                    for f in steps[slot]:
                        f()

            over_tiles(pool, body, lambda i: None)


def both_halves(dram_image):
    v = dram_image.rearrange("n c (h p) -> h (n c) p", h=2)
    return v[0], v[1]


def norm_stage(nc, xs, rec, x2, gn, consts):
    with ExitStack() as ctx:
        def sb(name, shape, dt=F32):
            return ctx.enter_context(nc.sbuf_tensor(name, shape, dt))

        def sem(name):
            return ctx.enter_context(nc.semaphore(name))

        HP = SIDE * SIDE // 2
        rows = [sb(f"n_rows{n}", [P, HP]) for n in range(2)]
        res = [sb(f"n_res{n}", [P, HP]) for n in range(2)]
        colp = sb("n_cols", [P, HP])
        stats = sb("n_stats", [P, HP // HALF, 6])
        mv = sb("n_mv", [P, 2])
        ms = sb("n_ms", [P, 2])
        gm = sb("n_gm", [P, 2])
        nv = sb("n_nv", [P, 1])
        sd = sb("n_sd", [P, 1])
        rs = sb("n_rs", [P, 1])
        scale = sb("n_scale", [P, 2])
        ma = sb("n_ma", [P, 2])
        shift = sb("n_shift", [P, 2])
        gnt = sb("n_gn", [P, 2])
        avg = sb("n_avg", [P, P])
        mean_ps = ctx.enter_context(nc.psum_tensor("n_mean", [P, 2], F32))

        s_w = sem("gn_weights_loaded")
        s_rowx = [sem("norm_rows_loaded0"), sem("norm_rows_loaded1")]
        s_col = sem("norm_cols_loaded")
        s_sum = sem("norm_summed")
        s_bn = sem("norm_chain")
        s_mean = sem("norm_group_mean")
        s_shift = sem("norm_affine_ready")
        s_sd = sem("norm_root")
        s_act = sem("norm_silu")
        s_res = sem("norm_residual")
        s_out = sem("norm_stored")
        CHAIN = 9

        block = ctx.enter_context(nc.Block())

        def over_images(engine, image):
            for b in range(BATCH):
                image(b, b % 2)

        @block.sync
        def _(sp):
            sp.dma_start(gnt[:, :], gn).then_inc(s_w, 16)
            sp.dma_start(avg[:, :], consts[:, 0:P]).then_inc(s_w, 16)

            def load(b, n):
                at_least(sp, s_out, 32 * (b - 1))
                for src, dst in ((rec, rows[n]), (xs, res[n])):
                    for h in range(2):
                        sp.dma_start(dst[64 * h:64 * h + 64, :].rearrange("c (t p) -> c t p", p=PX),
                                     src[bass.ds(b * 16 + 8 * h, 8)].rearrange("t c p -> c t p")
                                     ).then_inc(s_rowx[n], 16)
                at_least(sp, s_sum, b)
                for h in range(2):
                    dst = colp[64 * h:64 * h + 64, :].rearrange("c (t r p) -> c t r p", r=SEQS, p=64)
                    src = rec[bass.ds(TILES + b * 16, 16)].rearrange("t c (r p) -> c t r p", p=SIDE)
                    for t in range(16):
                        sp.dma_start(dst[:, t], src[:, t, :, 64 * h:64 * h + 64]).then_inc(s_col, 16)

            def store(b, n):
                sp.wait_ge(s_res, b + 1)
                for h, dst in enumerate(both_halves(x2[bass.ds(b, 1)])):
                    sp.dma_start(dst, res[n][64 * h:64 * h + 64, :]).then_inc(s_out, 16)

            load(0, 0)
            load(1, 1)
            for b in range(BATCH):
                store(b, b % 2)
                if b + 2 < BATCH:
                    load(b + 2, b % 2)
            sp.wait_ge(s_out, 32 * BATCH)

        @block.vector
        def _(dve):
            def image(b, n):
                c = CHAIN * b
                dve.wait_ge(s_rowx[n], 32 * (b - n) + 64)
                dve.wait_ge(s_col, 16 * 32 * (b + 1))
                nc.vector.tensor_tensor(rows[n][:, :].rearrange("p (h w) -> p h w", w=SIDE),
                                        rows[n][:, :].rearrange("p (h w) -> p h w", w=SIDE),
                                        colp[:, :].rearrange("p (w h) -> p h w", w=SIDE),
                                        ALU.add).then_inc(s_sum, 1)
                dve.wait_ge(s_sum, b + 1)
                for t in range(HP // HALF):
                    ins = nc.vector.bn_stats(stats[:, t, :], rows[n][:, t * HALF:(t + 1) * HALF])
                ins.then_inc(s_bn, 1)
                dve.wait_ge(s_bn, c + 1)
                nc.vector.bn_aggr(mv[:, :], stats[:, :, :]).then_inc(s_bn, 1)
                dve.wait_ge(s_bn, c + 2)
                nc.vector.tensor_copy(ms[:, 0:1], mv[:, 0:1])
                nc.vector.scalar_tensor_tensor(out=ms[:, 1:2], in0=mv[:, 0:1], scalar=mv[:, 0:1],
                                               in1=mv[:, 1:2], op0=ALU.mult, op1=ALU.add).then_inc(s_bn, 1)
                dve.wait_ge(s_mean, b + 1)
                nc.vector.tensor_copy(gm[:, :], mean_ps[:, :]).then_inc(s_bn, 1)
                dve.wait_ge(s_bn, c + 4)
                nc.vector.scalar_tensor_tensor(out=nv[:, :], in0=gm[:, 0:1], scalar=gm[:, 0:1],
                                               in1=gm[:, 1:2], op0=ALU.mult, op1=ALU.subtract).then_inc(s_bn, 1)
                dve.wait_ge(s_bn, c + 5)
                nc.vector.tensor_scalar(nv[:, :], nv[:, :], -1.0 / 16, EPS, ALU.mult,
                                        ALU.add).then_inc(s_bn, 1)
                dve.wait_ge(s_sd, b + 1)
                nc.vector.reciprocal(rs[:, :], sd[:, :]).then_inc(s_bn, 1)
                dve.wait_ge(s_bn, c + 7)
                at_least(dve, s_act, b - 1)
                nc.vector.scalar_tensor_tensor(out=scale[:, n:n + 1], in0=rs[:, :], scalar=0.25,
                                               in1=gnt[:, 0:1], op0=ALU.mult, op1=ALU.mult).then_inc(s_bn, 1)
                dve.wait_ge(s_bn, c + 8)
                nc.vector.tensor_tensor(ma[:, n:n + 1], gm[:, 0:1], scale[:, n:n + 1],
                                        ALU.mult).then_inc(s_bn, 1)
                dve.wait_ge(s_bn, c + 9)
                nc.vector.tensor_tensor(shift[:, n:n + 1], gnt[:, 1:2], ma[:, n:n + 1],
                                        ALU.subtract).then_inc(s_shift, 1)
                dve.wait_ge(s_act, b + 1)
                nc.vector.tensor_tensor(res[n][:, :], res[n][:, :], rows[n][:, :],
                                        ALU.add).then_inc(s_res, 1)
            dve.wait_ge(s_w, 32)
            over_images(dve, image)

        @block.tensor
        def _(pe):
            pe.wait_ge(s_w, 32)

            def image(b, n):
                pe.wait_ge(s_bn, CHAIN * b + 3)
                nc.tensor.matmul(mean_ps[:, :], avg[:, :], ms[:, :], start=True,
                                 stop=True).then_inc(s_mean, 1)
            over_images(pe, image)

        @block.scalar
        def _(act):
            def image(b, n):
                act.wait_ge(s_bn, CHAIN * b + 6)
                nc.scalar.activation(sd[:, :], nv[:, :], ACT.Sqrt).then_inc(s_sd, 1)
                act.wait_ge(s_shift, b + 1)
                nc.scalar.activation(rows[n][:, :], rows[n][:, :], ACT.Silu, bias=shift[:, n:n + 1],
                                     scale=scale[:, n:n + 1]).then_inc(s_act, 1)
            over_images(act, image)


def weight_stage(nc, p_weight, origin, new_param, consts, w_conv):
    CO = 8
    CHUNK = CO * CH * KTAPS
    CHUNKS = KSIZE // CHUNK
    with ExitStack() as ctx:
        def sb(name, shape, dt=F32):
            return ctx.enter_context(nc.sbuf_tensor(name, shape, dt))

        def sem(name):
            return ctx.enter_context(nc.semaphore(name))

        keys = [sb(f"w_keys{n}", [KEYS + 1, CHUNK]) for n in range(2)]
        par = sb("w_par", [KEYS + 1, 2])
        raw = sb("w_raw", [P, 2 * CHUNKS, CO // 2, KTAPS])
        made = [ctx.enter_context(nc.psum_tensor(f"w_made{n}", [P, HALF], F32)) for n in range(2)]
        s_par = sem("param_loaded")
        s_keys = [sem("keys_loaded0"), sem("keys_loaded1")]
        s_made = sem("weights_made")
        s_raw = sem("weights_copied")
        s_laid = sem("weights_laid_out")
        block = ctx.enter_context(nc.Block())

        def over_chunks(engine, chunk):
            chunk(0, 0, 0)
            chunk(1, 1, 0)
            with engine.Fori(1, CHUNKS // 2) as i:
                for n in range(2):
                    chunk(2 * i + n, n, 0)
            with engine.Fori(CHUNKS // 2, CHUNKS) as i:
                for n in range(2):
                    chunk(2 * i + n, n, 1)

        @block.sync
        def _(sp):
            for c in range(2):
                sp.dma_start(par[0:KEYS, c:c + 1], new_param).then_inc(s_par, 16)
            sp.dma_start(par[KEYS:KEYS + 1, 0:1], consts[0:1, 2 * P:2 * P + 1]).then_inc(s_par, 16)
            sp.dma_start(par[KEYS:KEYS + 1, 1:2], new_param[KEYS - 1:KEYS, :]).then_inc(s_par, 16)

            def chunk(m, n, c):
                at_least(sp, s_made, m - 1)
                at = bass.ds(m * CHUNK, CHUNK)
                sp.dma_start(keys[n][0:KEYS, :], p_weight[:, at]).then_inc(s_keys[n], 16)
                sp.dma_start(keys[n][KEYS:KEYS + 1, :], origin[:, at]).then_inc(s_keys[n], 16)
            over_chunks(sp, chunk)

        @block.tensor
        def _(pe):
            pe.wait_ge(s_par, 64)

            def chunk(m, n, c):
                pe.wait_ge(s_keys[n], 16 * (m - n) + 32)
                at_least(pe, s_raw, m - 1)
                k = keys[n][:, :].rearrange("k (o q i t) -> k o t q i", q=2, i=CH, t=KTAPS)
                for o in range(CO // 2):
                    for t in range(KTAPS):
                        col = o * KTAPS + t
                        mm = nc.tensor.matmul(made[n][:, col:col + 1], k[:, o, t], par[:, c:c + 1],
                                              start=True, stop=True)
                mm.then_inc(s_made, 1)
            over_chunks(pe, chunk)

        @block.vector
        def _(dve):
            for c in range(2):
                nc.vector.memset(w_conv[c][:, :, :], 0.0).then_inc(s_laid, 1)

            def chunk(m, n, c):
                dve.wait_ge(s_made, m + 1)
                nc.vector.tensor_copy(raw[:, bass.ds(m, 1), :, :].rearrange("p m o t -> p (m o t)"),
                                      made[n][:, 0:CO // 2 * KTAPS]).then_inc(s_raw, 1)
            over_chunks(dve, chunk)
            dve.wait_ge(s_raw, 2 * CHUNKS)
            dve.wait_ge(s_laid, 2)
            for c in range(2):
                for q in range(2):
                    src = raw[64 * q:64 * q + 64, c * CHUNKS:(c + 1) * CHUNKS].rearrange(
                        "p m o t -> p t (m o)")
                    for dy, rows, m0 in ((0, 0, 0), (1, 64, 0), (2, 0, 3)):
                        dst = w_conv[c][rows:rows + 64, m0:m0 + 3, :].rearrange(
                            "p d (o q) -> p d o q", q=2)[:, :, :, q]
                        nc.vector.tensor_copy(dst, src[:, 3 * dy:3 * dy + 3, :]).then_inc(s_laid, 1)
            dve.wait_ge(s_laid, 14)


def conv_stage(nc, tag, src, dst, w, affine, bn, consts, out_affine):
    with ExitStack() as ctx:
        def sb(name, shape, dt=F32):
            return ctx.enter_context(nc.sbuf_tensor(f"{tag}_{name}", shape, dt))

        def sem(name):
            return ctx.enter_context(nc.semaphore(f"{tag}_{name}"))

        W = SIDE + 2
        BLOCKS = 16
        img = [sb(f"img{n}", [P, W, W]) for n in range(2)]
        out = sb("out", [P, 2, 4 * HALF])
        stats = sb("stats", [P, BATCH * BLOCKS, 6])
        mv = sb("mv", [P, 2])
        ms = sb("ms", [P, 2])
        gm = sb("gm", [P, 2])
        nv = sb("nv", [P, 1])
        sd = sb("sd", [P, 1])
        rs = sb("rs", [P, 1])
        ma = sb("ma", [P, 1])
        bnt = sb("bn", [P, 2])
        avg = sb("avg", [P, P])
        acc = [ctx.enter_context(nc.psum_tensor(f"{tag}_acc{n}", [P, HALF], F32)) for n in range(8)]

        s_w = sem("weights_loaded")
        s_zero = sem("borders_zero")
        s_img = [sem("image_loaded0"), sem("image_loaded1")]
        s_pre = sem("image_activated")
        s_conv = sem("block_convolved")
        s_copy = sem("block_copied")
        s_stat = sem("block_measured")
        s_out = [sem("quarter_stored0"), sem("quarter_stored1")]
        s_chain = sem("chain")
        s_mean = sem("mean")
        s_sd = sem("root")
        block = ctx.enter_context(nc.Block())

        def over_images(engine, image):
            image(0, 0)
            image(1, 1)
            with engine.Fori(1, BATCH // 2) as i:
                image(2 * i, 0)
                image(2 * i + 1, 1)

        def body_of(n, half):
            rows = slice(1, 1 + SIDE) if half == 0 else slice(0, SIDE)
            return img[n][64 * half:64 * half + 64, rows, 1:1 + SIDE]

        @block.sync
        def _(sp):
            sp.dma_start(bnt[:, :], bn).then_inc(s_w, 16)
            sp.dma_start(avg[:, :], consts[:, P:2 * P]).then_inc(s_w, 16)
            sp.wait_ge(s_zero, 2)

            def load(b, n):
                at_least(sp, s_conv, BLOCKS * (b - 1))
                for half in range(2):
                    sp.dma_start(body_of(n, half),
                                 src[bass.ds(b, 1)].rearrange("n c (h w) -> (n c) h w", w=SIDE)
                                 ).then_inc(s_img[n], 16)

            def store(b):
                for q in range(4):
                    sp.wait_ge(s_copy, BLOCKS * b + 4 * q + 4)
                    sp.wait_ge(s_stat, BLOCKS * b + 4 * q + 4)
                    for h, half in enumerate(both_halves(dst[bass.ds(b, 1)])):
                        sp.dma_start(half[:, 4 * q * HALF:4 * (q + 1) * HALF],
                                     out[64 * h:64 * h + 64, q % 2, :]).then_inc(s_out[q % 2], 16)

            load(0, 0)
            load(1, 1)
            with sp.Fori(0, BATCH // 2 - 1) as i:
                for n in range(2):
                    store(2 * i + n)
                    load(2 * i + 2 + n, n)
            store(BATCH - 2)
            store(BATCH - 1)
            for n in range(2):
                sp.wait_ge(s_out[n], 64 * BATCH)

        @block.tensor
        def _(pe):
            pe.wait_ge(s_w, 32)

            def image(b, n):
                if affine is None:
                    pe.wait_ge(s_img[n], 16 * (b - n) + 32)
                else:
                    pe.wait_ge(s_pre, 2 * b + 2)
                for m in range(BLOCKS):
                    at_least(pe, s_copy, BLOCKS * b + m - 7)
                    for t in range(6):
                        dy, dx = (0, t) if t < 3 else (2, t - 3)
                        for h in range(2):
                            y = 64 * h + 4 * m + dy
                            mm = nc.tensor.matmul(acc[m % 8][64 * h:64 * h + 64, :], w[:, t, :],
                                                  img[n][:, y:y + 4, dx:dx + SIDE],
                                                  start=(t == 0), stop=(t == 5),
                                                  tile_position=(0, 64 * h))
                    mm.then_inc(s_conv, 1)
            over_images(pe, image)
            pe.wait_ge(s_chain, 3)
            nc.tensor.matmul(acc[0][:, 0:2], avg[:, :], ms[:, :], start=True, stop=True).then_inc(s_mean, 1)

        @block.scalar
        def _(act):
            def activate(b, n):
                if affine is None:
                    return
                act.wait_ge(s_img[n], 16 * (b - n) + 32)
                for half in range(2):
                    v = body_of(n, half)
                    rows = slice(64 * half, 64 * half + 64)
                    nc.scalar.activation(v, v, ACT.Relu, bias=affine[rows, 1:2],
                                         scale=affine[rows, 0:1]).then_inc(s_pre, 1)

            def image(b, n):
                for m in range(BLOCKS):
                    if m == 4:
                        later(b + 1, 1 - n)
                    act.wait_ge(s_conv, BLOCKS * b + m + 1)
                    if m % 4 == 0:
                        at_least(act, s_out[m // 4 % 2], 64 * b + 32 * (m // 8))
                    nc.scalar.copy(out[:, m // 4 % 2, (m % 4) * HALF:(m % 4 + 1) * HALF],
                                   acc[m % 8][:, :]).then_inc(s_copy, 1)

            later = activate
            activate(0, 0)
            image(0, 0)
            image(1, 1)
            with act.Fori(1, BATCH // 2 - 1) as i:
                image(2 * i, 0)
                image(2 * i + 1, 1)
            image(BATCH - 2, 0)
            later = lambda b, n: None
            image(BATCH - 1, 1)
            act.wait_ge(s_chain, 6)
            nc.scalar.activation(sd[:, :], nv[:, :], ACT.Sqrt).then_inc(s_sd, 1)

        @block.vector
        def _(dve):
            for n in range(2):
                nc.vector.memset(img[n][:, :, :], 0.0).then_inc(s_zero, 1)
            dve.wait_ge(s_w, 32)

            def image(b, n):
                for m in range(BLOCKS):
                    dve.wait_ge(s_copy, BLOCKS * b + m + 1)
                    nc.vector.bn_stats(stats[:, bass.ds(b * BLOCKS + m, 1), :].rearrange("p o s -> p (o s)"),
                                       out[:, m // 4 % 2, (m % 4) * HALF:(m % 4 + 1) * HALF]
                                       ).then_inc(s_stat, 1)
            over_images(dve, image)
            dve.wait_ge(s_stat, BATCH * BLOCKS)
            nc.vector.bn_aggr(mv[:, :], stats[:, :, :]).then_inc(s_chain, 1)
            dve.wait_ge(s_chain, 1)
            nc.vector.tensor_copy(ms[:, 0:1], mv[:, 0:1]).then_inc(s_chain, 1)
            nc.vector.scalar_tensor_tensor(out=ms[:, 1:2], in0=mv[:, 0:1], scalar=mv[:, 0:1],
                                           in1=mv[:, 1:2], op0=ALU.mult, op1=ALU.add).then_inc(s_chain, 1)
            dve.wait_ge(s_mean, 1)
            nc.vector.tensor_copy(gm[:, :], acc[0][:, 0:2]).then_inc(s_chain, 1)
            dve.wait_ge(s_chain, 4)
            nc.vector.scalar_tensor_tensor(out=nv[:, :], in0=gm[:, 0:1], scalar=gm[:, 0:1],
                                           in1=gm[:, 1:2], op0=ALU.mult, op1=ALU.subtract).then_inc(s_chain, 1)
            dve.wait_ge(s_chain, 5)
            nc.vector.tensor_scalar(nv[:, :], nv[:, :], -1.0, EPS, ALU.mult, ALU.add).then_inc(s_chain, 1)
            dve.wait_ge(s_sd, 1)
            nc.vector.reciprocal(rs[:, :], sd[:, :]).then_inc(s_chain, 1)
            dve.wait_ge(s_chain, 7)
            nc.vector.tensor_tensor(out_affine[:, 0:1], rs[:, :], bnt[:, 0:1], ALU.mult).then_inc(s_chain, 1)
            dve.wait_ge(s_chain, 8)
            nc.vector.tensor_tensor(ma[:, :], gm[:, 0:1], out_affine[:, 0:1], ALU.mult).then_inc(s_chain, 1)
            dve.wait_ge(s_chain, 9)
            nc.vector.tensor_tensor(out_affine[:, 1:2], bnt[:, 1:2], ma[:, :], ALU.subtract).then_inc(s_chain, 1)
            dve.wait_ge(s_chain, 10)


def end_stage(nc, y2, x2, out, affine):
    with ExitStack() as ctx:
        def sem(name):
            return ctx.enter_context(nc.semaphore(name))

        HP = SIDE * SIDE // 2
        y = [ctx.enter_context(nc.sbuf_tensor(f"e_y{n}", [P, HP], F32)) for n in range(2)]
        x = [ctx.enter_context(nc.sbuf_tensor(f"e_x{n}", [P, HP], F32)) for n in range(2)]
        s_in = [sem("end_loaded0"), sem("end_loaded1")]
        s_add = sem("end_added")
        s_relu = sem("end_relu")
        s_out = sem("end_stored")
        block = ctx.enter_context(nc.Block())

        def over_images(engine, image):
            image(0, 0)
            image(1, 1)
            with engine.Fori(1, BATCH // 2) as i:
                image(2 * i, 0)
                image(2 * i + 1, 1)

        @block.sync
        def _(sp):
            def load(b, n):
                at_least(sp, s_out, 32 * (b - 1))
                for src, dst in ((y2, y[n]), (x2, x[n])):
                    for h, half in enumerate(both_halves(src[bass.ds(b, 1)])):
                        sp.dma_start(dst[64 * h:64 * h + 64, :], half).then_inc(s_in[n], 16)

            def store(b, n):
                sp.wait_ge(s_relu, b + 1)
                for h, half in enumerate(both_halves(out[bass.ds(b, 1)])):
                    sp.dma_start(half, y[n][64 * h:64 * h + 64, :]).then_inc(s_out, 16)

            load(0, 0)
            load(1, 1)
            with sp.Fori(0, BATCH // 2 - 1) as i:
                for n in range(2):
                    store(2 * i + n, n)
                    load(2 * i + 2 + n, n)
            store(BATCH - 2, 0)
            store(BATCH - 1, 1)
            sp.wait_ge(s_out, 32 * BATCH)

        @block.vector
        def _(dve):
            def image(b, n):
                dve.wait_ge(s_in[n], 32 * (b - n) + 64)
                nc.vector.scalar_tensor_tensor(out=y[n][:, :], in0=y[n][:, :], scalar=affine[:, 0:1],
                                               in1=x[n][:, :], op0=ALU.mult, op1=ALU.add).then_inc(s_add, 1)
            over_images(dve, image)

        @block.scalar
        def _(act):
            def image(b, n):
                act.wait_ge(s_add, b + 1)
                nc.scalar.activation(y[n][:, :], y[n][:, :], ACT.Relu, bias=affine[:, 1:2]).then_inc(s_relu, 1)
            over_images(act, image)


def build(nc, a, out):
    sets = [{k: a[f"{k}_{s}"] for k in ("in_t", "conv_t", "xp_t", "xp_dt", "dt_t", "out_t", "a_log", "cols")}
            for s in ("row", "col")]
    rec = nc.dram_tensor("rec", (2 * TILES, CH, PX), F32, kind="Internal").ap()
    x2 = nc.dram_tensor("x2", (BATCH, CH, SIDE * SIDE), F32, kind="Internal").ap()
    y1 = nc.dram_tensor("y1", (BATCH, CH, SIDE * SIDE), F32, kind="Internal").ap()
    y2 = nc.dram_tensor("y2", (BATCH, CH, SIDE * SIDE), F32, kind="Internal").ap()
    scan_stage(nc, a["xs"], rec, sets, a["select"])
    norm_stage(nc, a["xs"], rec, x2, a["gn"], a["average"])
    with ExitStack() as ctx:
        w_conv = [ctx.enter_context(nc.sbuf_tensor(f"w_conv{c}", [P, 6, CH], F32)) for c in range(2)]
        affine = [ctx.enter_context(nc.sbuf_tensor(f"affine{c}", [P, 2], F32)) for c in range(2)]
        weight_stage(nc, a["p_weight"], a["origin"], a["new_param"], a["average"], w_conv)
        conv_stage(nc, "c1", x2, y1, w_conv[0], None, a["bn1"], a["average"], affine[0])
        conv_stage(nc, "c2", y1, y2, w_conv[1], affine[0], a["bn2"], a["average"], affine[1])
        end_stage(nc, y2, x2, out, affine[1])


def kernel(**inputs):
    import numpy as np
    import concourse.bacc as bacc
    from concourse.bass_utils import run_bass_kernel_spmd

    def arr(name):
        return np.asarray(inputs[name])

    def tiles_of(x):
        return x.reshape(BATCH, CH, SIDE // SEQS, SEQS, SIDE).transpose(0, 2, 1, 3, 4).reshape(-1, CH, PX)

    x = arr("x")
    arrays = {"xs": np.concatenate([tiles_of(x), tiles_of(x.transpose(0, 1, 3, 2))])}
    for s in ("row", "col"):
        w = {k: arr(f"L0_conv_{s}_{k}") for k in
             ("in_w", "conv_w", "conv_b", "xp_w", "dt_w", "dt_b", "A_log", "D", "out_w")}
        arrays[f"in_t_{s}"] = w["in_w"].T
        arrays[f"conv_t_{s}"] = w["conv_w"][:, 0, :].T
        arrays[f"xp_t_{s}"] = w["xp_w"].T
        arrays[f"xp_dt_{s}"] = w["xp_w"][:DTR]
        arrays[f"dt_t_{s}"] = w["dt_w"].T
        arrays[f"out_t_{s}"] = w["out_w"].T
        arrays[f"a_log_{s}"] = w["A_log"].reshape(GROUPS, 8, NS).transpose(2, 1, 0).reshape(P, GROUPS)
        arrays[f"cols_{s}"] = np.stack([w["conv_b"], w["dt_b"], w["D"]], 1)
    twice = lambda p, q: np.concatenate([np.stack([arr(p), arr(q)], 1)] * 2)
    arrays["gn"] = twice("L0_conv_gn_w", "L0_conv_gn_b")
    arrays["bn1"] = twice("L1_conv_bn1_gamma", "L1_conv_bn1_beta")
    arrays["bn2"] = twice("L1_conv_bn2_gamma", "L1_conv_bn2_beta")
    arrays["p_weight"] = arr("L1_conv_P_weight")
    arrays["origin"] = arr("L1_conv_origin_weight")[None, :]
    arrays["new_param"] = arr("L1_conv_new_param")[:, None]

    select = np.zeros((P, 4 * P + 4 * 32), np.float32)
    for k in range(4):
        for r in range(8):
            for n in range(NS):
                for part in range(3):
                    select[32 * part + 8 * k + r, P * k + 8 * n + r] = 1
                select[8 * n + r, 4 * P + 32 * k + 8 * k + r] = 1
    arrays["select"] = select
    average = np.zeros((P, 2 * P + 1), np.float32)
    ch = np.arange(P) % CH
    per = CH // GN_GROUPS
    average[:, 0:P] = (ch[:, None] // per == ch[None, :] // per) / (2.0 * per)
    average[:, P:2 * P] = (ch[:, None] == ch[None, :]) / 2.0
    average[:, 2 * P] = 1
    arrays["average"] = average

    nc = bacc.Bacc("TRN2", target_bir_lowering=False, num_devices=1)
    arrays = {f"in_{k}": np.ascontiguousarray(v) for k, v in arrays.items()}
    aps = {k[3:]: nc.dram_tensor(k, v.shape, F32, kind="ExternalInput").ap() for k, v in arrays.items()}
    out = nc.dram_tensor("out", (BATCH, CH, SIDE * SIDE), F32, kind="ExternalOutput").ap()
    build(nc, aps, out)
    r = run_bass_kernel_spmd(nc, [arrays], core_ids=[0])
    return r.results[0]["out"].reshape(BATCH, CH, SIDE, SIDE)
```

```python
from contextlib import ExitStack

import concourse.bass as bass
from concourse import mybir

F32 = mybir.dt.float32
BF16 = mybir.dt.bfloat16
ALU = mybir.AluOpType
ACT = mybir.ActivationFunctionType

P = 128
BATCH, CH, SIDE = 8, 64, 128
DI, NS, DTR, TAPS = 128, 16, 4, 4
SEQS = 8
PX = SEQS * SIDE
HALF = 512
PAD = SIDE + 2 * (TAPS - 1)
TILES = BATCH * SIDE // SEQS
GROUPS = DI // 8
UNIT = 2 * GROUPS
SLOTS = 2 * UNIT
YB = SLOTS // 4
LEAD = 5
STEPS = 20
FIRST_STEPS = 10
STACK_DMAS = 24
FWD, REV = 0, 1
A_RING, H_RING, C_RING = 8, 4, 16
GN_GROUPS, EPS = 4, 1e-5
KEYS = 40
KTAPS = 9
KSIZE = CH * CH * KTAPS


def at_least(engine, semaphore, value):
    if isinstance(value, int) and value <= 0:
        return
    engine.wait_ge(semaphore, value)


def group_of(slot):
    d, q = divmod(slot, UNIT)
    half, r = divmod(q, GROUPS)
    k, j = divmod(r, 4)
    return d, half, k, j


def du_bank_before(slot):
    return {0: 2, 1: 2, 2: 5}.get(slot % UNIT, 3)


def steps_before(i, first):
    return FIRST_STEPS if first else FIRST_STEPS - 1 + STEPS * i


class Step:

    def __init__(self, pe, act, kind, d, half, weights):
        self.pe, self.act, self.kind, self.d, self.half, self.weights = pe, act, kind, d, half, weights


PROJECT = ((1, 5, "dt", 0),
           (1, 8, "dt", 1),
           (3, 12, "b", 0),
           (7, 12, "b", 1),
           (9, 16, "c", 0),
           (10, 16, "c", 1))
OUT_1, OUT_0 = (12, 19), (55, 60)
X_FWD, X_REV = ((26, 27), (29, 30)), ((58, 59), (59, 61))
Z = (18, 19)
ADD_UD, ADD_FWD = (15, 30, 45, 59), (49, 63)
SUM = (8, 12, 16, 20, 24, 28, 32, 36, 40, 44, 48, 52, 56, 60, 64, 68)
TWO, NONE = (13, 25, 46, 62), (17, 24, 48, 60)
SILU_Z, SILU_FWD, SILU_REV = 25, 36, 3
TAKE_FWD = (26, 43)
SOFTPLUS, HIGH, MIDDLE = (9, 10, 11), (19, 20), (22, 24)
GATE_1, GATE_0 = 5, 52
CORRECT, DELTA_AT, DU_AT, REST = 8, 10, 12, (15, 16)
LOG, LOW = 6, (15, 17)


def plan(prev, cur, nxt):
    def project(base, d, w):
        return [Step(base + pe, base + act, kind, d, half, w) for pe, act, kind, half in PROJECT]

    steps = project(0, REV, cur)
    if prev is not None:
        steps.append(Step(*OUT_1, "out", REV, 1, prev))
    steps += [Step(Z[h], SILU_Z, "z", FWD, h, cur) for h in range(2)]
    if nxt is not None:
        steps += [Step(X_FWD[h][1], SILU_FWD, "x", FWD, h, nxt) for h in range(2)]
    if nxt is not None:
        steps += project(UNIT, FWD, nxt)
    steps.append(Step(*OUT_0, "out", REV, 0, cur))
    if nxt is not None:
        steps += [Step(X_REV[h][1], SLOTS + SILU_REV, "x", REV, h, nxt) for h in range(2)]
    last = {0: -2, 1: -1}
    for n, step in enumerate(steps):
        step.n, step.bank = n, 0 if last[0] < last[1] else 1
        if prev is None and step.kind == "z" and step.half == 0:
            step.bank = 1
        step.free = last[step.bank] + 1
        last[step.bank] = n
    return steps


def scan_stage(nc, xs, rec, weights, consts):
    with ExitStack() as ctx:
        def sb(name, shape, dt=F32):
            return ctx.enter_context(nc.sbuf_tensor(name, shape, dt))

        def pb(name, shape):
            return ctx.enter_context(nc.psum_tensor(name, shape, F32))

        def sem(name):
            return ctx.enter_context(nc.semaphore(name))

        in_t = [sb(f"in_t{s}", [P, 2 * DI]) for s in range(2)]
        taps = [sb(f"taps{s}", [P, 4, DI]) for s in range(2)]
        xp_t = [sb(f"xp_t{s}", [P, DTR + 2 * NS]) for s in range(2)]
        xp_dt = [sb(f"xp_dt{s}", [DTR, DI]) for s in range(2)]
        dt_t = [sb(f"dt_t{s}", [DTR, DI]) for s in range(2)]
        to_b = [sb(f"to_b{s}", [P, P]) for s in range(2)]
        to_c = [sb(f"to_c{s}", [P, P]) for s in range(2)]
        to_dt = [sb(f"to_dt{s}", [P, P]) for s in range(2)]
        out_t = [sb(f"out_t{s}", [P, CH]) for s in range(2)]
        a_neg = [sb(f"a_neg{s}", [P, GROUPS]) for s in range(2)]
        cols = [sb(f"cols{s}", [P, 3]) for s in range(2)]
        d_diag = [sb(f"d_diag{s}", [P, P]) for s in range(2)]
        sel_f = sb("sel_f", [P, 4 * P + 4 * 32 + P])
        spread = sb("spread", [P, 4, P], BF16)
        gather = sel_f[:, 4 * P:5 * P].rearrange("p (k m) -> p k m", k=4)

        xt = sb("xt", [P, SEQS, PAD])
        xz = sb("xz", [CH, PX])
        u = [sb(f"u{d}", [P, PX]) for d in range(2)]
        zs = sb("zs", [P, PX])
        b_rep = [sb(f"b_rep{d}", [P, PX]) for d in range(2)]
        c_rep = [sb(f"c_rep{d}", [P, PX]) for d in range(2)]
        expabs = sb("expabs", [P, PX])
        onep = sb("onep", [P, PX])
        delta = sb("delta", [P, PX])
        vpos = sb("vpos", [P, PX])
        du = expabs
        d_parts = [sb(f"d_parts{d}", [P, 3, PX], BF16) for d in range(2)]
        u_parts = sb("u_parts", [P, 3, PX], BF16)
        d_stack = [sb(f"d_stack{d}", [96, 4, PX], BF16) for d in range(2)]
        u_stack = [sb(f"u_stack{d}", [96, 4, PX], BF16) for d in range(2)]
        decay = [sb(f"decay{d}", [P, A_RING, HALF]) for d in range(2)]
        state = sb("state", [P, H_RING, HALF])
        read = sb("read", [P, C_RING, HALF])
        y_fwd = sb("y_fwd", [P, PX])
        gated = sb("gated", [P, 2, HALF])
        o_sb = sb("o_sb", [CH, 2, HALF])

        d_bank = [pb(f"d_bank{n}", [P, HALF]) for n in range(2)]
        u_bank = [pb(f"u_bank{n}", [P, HALF]) for n in range(3)]
        y_bank = pb("y_bank", [P, HALF])
        p_bank = [pb(f"p_bank{n}", [P, HALF]) for n in range(2)]

        s_load = sem("weights_loaded")
        s_prep = sem("weights_prepared")
        s_dtw = sem("dt_weights_multiplied")
        s_exp_a = sem("a_exponentiated")
        s_x = sem("x_loaded")
        s_xz = sem("x_for_z_loaded")
        s_delta_b = sem("delta_spread")
        s_du_b = sem("du_spread")
        s_decay = sem("decay_ready")
        s_drive = sem("drive_ready")
        s_state = sem("state_ready")
        s_read = sem("read_ready")
        s_ysum = sem("y_batch_summed")
        s_ud = sem("u_times_d_added")
        s_yf = sem("y_forward_taken")
        s_yf_used = sem("y_forward_added")
        s_gate = sem("gated_ready")
        s_proj = sem("projection_ready")
        s_evac = sem("projection_taken")
        s_soft = sem("softplus_parts")
        s_delta = sem("delta_steps")
        s_ln = sem("log_corrected")
        s_hi = sem("high_parts")
        s_rest = sem("rests")
        s_mid = sem("middle_parts")
        s_low = sem("low_parts")
        s_stack = sem("stacked")
        s_store = sem("rec_stored")

        n_load = 0

        def seqs(ap):
            return ap.rearrange("p (s t) -> p s t", t=SIDE)

        def inner(ap, d):
            v = seqs(ap)
            return v[:, :, 1:SIDE] if d == FWD else v[:, :, 0:SIDE - 1]

        def first(ap, d):
            v = seqs(ap)
            return v[:, :, 0:1] if d == FWD else v[:, :, SIDE - 1:SIDE]

        def px(h):
            return slice(h * HALF, (h + 1) * HALF)

        def tail_start(i):
            return steps_before(i - 1, False) + len(plan(1, 1, None))

        spread_before = [LEAD]
        for slot in range(SLOTS):
            spread_before.append(spread_before[-1] + 1 + TWO.count(slot) - NONE.count(slot))

        block = ctx.enter_context(nc.Block())

        def over_tiles(engine, body, tail):
            body(0, 0, None, 0)
            with engine.Fori(1, TILES - 1) as i:
                body(i, 0, 0, 0)
            body(TILES - 1, 0, 0, 1)
            body(TILES, 1, 0, 1)
            with engine.Fori(TILES + 1, 2 * TILES - 1) as i:
                body(i, 1, 1, 1)
            body(2 * TILES - 1, 1, 1, None)
            tail(2 * TILES)

        @block.sync
        def _(sp):
            def load(dst, src):
                sp.dma_start(dst, src).then_inc(s_load, 16)

            for s in range(2):
                w = weights[s]
                for half in range(2):
                    load(in_t[s][64 * half:64 * half + 64, :], w["in_t"])
                for m, pair in enumerate(((3, 2), (1, 0), (2, 3), (0, 1))):
                    for half in range(2):
                        row = w["conv_t"][pair[half]:pair[half] + 1, :]
                        load(taps[s][64 * half:64 * half + 64, m, :],
                             bass.AP(row.tensor, row.offset, [[0, 64], [1, DI]]))
                load(xp_t[s][:, :], w["xp_t"])
                load(xp_dt[s][:, :], w["xp_dt"])
                load(dt_t[s][:, :], w["dt_t"])
                load(out_t[s][:, :], w["out_t"])
                load(a_neg[s][:, :], w["a_log"])
                load(cols[s][:, :], w["cols"])
            load(sel_f[:, :], consts)

            def load_x(tile):
                x = xs[bass.ds(tile, 1)].rearrange("n c (s t) -> (n c) s t", t=SIDE)
                sp.dma_start(xt[0:64, :, 3:3 + SIDE], x).then_inc(s_x, 16)
                sp.dma_start(xt[64:128, :, 4:4 + SIDE], x).then_inc(s_x, 16)

            def load_xz(tile):
                sp.dma_start(xz[:, :], xs[bass.ds(tile, 1)].rearrange("n c p -> (n c) p")
                             ).then_inc(s_xz, 16)

            def stack(unit, d, free_at):
                at_least(sp, s_du_b, free_at)
                at_least(sp, s_delta_b, free_at)
                for part, ready in ((0, s_hi), (1, s_mid), (2, s_low)):
                    for t, (parts, stacked) in enumerate(((d_parts[d], d_stack[d]),
                                                          (u_parts, u_stack[d]))):
                        sp.wait_ge(ready, unit * 2 + t + 1)
                        for j in range(4):
                            sp.dma_start(stacked[32 * part:32 * part + 32, j, :],
                                         parts[32 * j:32 * j + 32, part, :]).then_inc(s_stack, 16)

            def store(tile, half, count):
                sp.wait_ge(s_evac, count)
                dst = rec[bass.ds(tile, 1)].rearrange("n c p -> (n c) p")
                sp.dma_start(dst[:, px(half)], o_sb[:, half, :]).then_inc(s_store, 16)

            sp.wait_ge(s_prep, 1)
            load_x(0)
            stack(0, FWD, 0)

            def body(i, cur, prev, nxt):
                start = steps_before(i, prev is None)
                steps = plan(prev, cur, nxt)
                sp.wait_ge(s_proj, start)
                load_xz(i)
                if nxt is not None:
                    load_x(i + 1)
                for step in steps:
                    if step.kind == "out" and step.half == 1:
                        store(i - 1, 1, start + step.n + 1)
                stack(2 * i + 1, REV, SLOTS * i)
                if nxt is not None:
                    stack(2 * i + 2, FWD, SLOTS * i + UNIT)
                for step in steps:
                    if step.kind == "out" and step.half == 0:
                        store(i, 0, start + step.n + 1)

            def tail(i):
                store(i - 1, 1, tail_start(i) + 1)
                sp.wait_ge(s_store, 16 * 2 * i)

            over_tiles(sp, body, tail)

        N_LOAD = 16 * (2 * 16 + 1)
        BEFORE = ([("x", FWD, h) for h in range(2)]
                  + [(kind, FWD, h) for kind in ("dt", "b", "c") for h in range(2)]
                  + [("x", REV, h) for h in range(2)])

        @block.tensor
        def _(pe):
            pe.wait_ge(s_load, N_LOAD)
            for s in range(2):
                nc.tensor.matmul(p_bank[s][:, 0:P], xp_dt[s][:, :], dt_t[s][:, :],
                                 start=True, stop=True).then_inc(s_dtw, 1)

            def conv(bank, s, d, h, m):
                offs = (3, 1) if d == FWD else (4, 6)
                mm = nc.tensor.matmul(p_bank[bank][:, :], taps[s][:, 2 * d + m, :],
                                      xt[:, 4 * h:4 * h + 4, offs[m]:offs[m] + SIDE],
                                      start=(m == 0), stop=(m == 1))
                if m == 1:
                    mm.then_inc(s_proj, 1)

            def conv_first_half(step, i, start):
                at_least(pe, s_evac, start + step.free)
                if step.half == 0 and step.d == FWD:
                    pe.wait_ge(s_x, 32 * (i + 2))
                conv(step.bank, step.weights, step.d, step.half, 0)

            def project(bank, lhs, rhs, rows=P):
                nc.tensor.matmul(p_bank[bank][0:rows, :], lhs, rhs, start=True,
                                 stop=True).then_inc(s_proj, 1)

            def run(step, i, start, u_ready):
                s, h = step.weights, step.half
                if step.kind != "x":
                    at_least(pe, s_evac, start + step.free)
                if step.kind == "x":
                    conv(step.bank, s, step.d, h, 1)
                elif step.kind == "z":
                    if h == 0:
                        pe.wait_ge(s_xz, 16 * (i + 1))
                    project(step.bank, in_t[s][0:64, DI:2 * DI], xz[:, px(h)])
                elif step.kind == "out":
                    tile = i if h == 0 else i - 1
                    pe.wait_ge(s_gate, 2 * tile + h + 1)
                    project(step.bank, out_t[s][:, :], gated[:, h, :], CH)
                else:
                    if step.kind == "dt" and h == 0:
                        pe.wait_ge(s_evac, u_ready[step.d])
                    lhs = {"b": to_b, "c": to_c, "dt": to_dt}[step.kind][s]
                    project(step.bank, lhs[:, :], u[step.d][:, px(h)])

            def spread_delta(i, slot):
                d, half, k, j = group_of(slot)
                if slot % UNIT == 0:
                    pe.wait_ge(s_stack, 16 * STACK_DMAS * (2 * i + d + 1))
                at_least(pe, s_decay, SLOTS * i + slot - 1)
                nc.tensor.matmul(d_bank[slot % 2][:, :], spread[0:96, k, :],
                                 d_stack[d][:, j, px(half)], start=True,
                                 stop=True).then_inc(s_delta_b, 1)

            def spread_du(i, slot):
                d, half, k, j = group_of(slot)
                at_least(pe, s_state, SLOTS * i + slot - du_bank_before(slot) + 1)
                nc.tensor.matmul(u_bank[slot % UNIT % 3][:, :], spread[0:96, k, :],
                                 u_stack[d][:, j, px(half)], start=True,
                                 stop=True).then_inc(s_du_b, 1)

            def add_ud(i, e, s):
                nc.tensor.matmul(y_bank[:, :], d_diag[s][:, :], u[e // 2][:, px(e % 2)],
                                 start=False, stop=False, skip_group_check=True).then_inc(s_ud, 1)

            def add_forward(i, half):
                pe.wait_ge(s_yf, 2 * i + half + 1)
                nc.tensor.matmul(y_bank[:, :], sel_f[:, 5 * P:6 * P], y_fwd[:, px(half)],
                                 start=False, stop=False,
                                 skip_group_check=True).then_inc(s_yf_used, 1)

            def sum_batch(i, b):
                e, k = divmod(b, 4)
                if k == 0 and e in (0, 3):
                    at_least(pe, s_gate, 2 * i + (0 if e == 0 else 1))
                elif k == 0:
                    pe.wait_ge(s_yf, 2 * i + e)
                pe.wait_ge(s_read, SLOTS * i + 4 * b + 4)
                for j in range(4):
                    mm = nc.tensor.matmul(y_bank[32 * j:32 * j + 32, :], gather[:, k, :],
                                          read[:, (4 * b + j) % C_RING, :],
                                          start=(k == 0), stop=(k == 3),
                                          tile_position=(0, 32 * j), skip_group_check=True)
                mm.then_inc(s_ysum, 1)

            pe.wait_ge(s_prep, 4)
            pe.wait_ge(s_x, 32)
            for n, (kind, d, h) in enumerate(BEFORE):
                at_least(pe, s_evac, n - 1)
                if kind == "x":
                    conv(n % 2, 0, d, h, 0)
                    conv(n % 2, 0, d, h, 1)
                else:
                    pe.wait_ge(s_evac, 2)
                    lhs = {"b": to_b, "c": to_c, "dt": to_dt}[kind][0]
                    project(n % 2, lhs[:, :], u[d][:, px(h)])
            for slot in range(LEAD):
                spread_delta(0, slot)

            def body(i, cur, prev, nxt):
                start = steps_before(i, prev is None)
                steps = plan(prev, cur, nxt)
                u_ready = {REV: start}
                for step in steps:
                    if step.kind == "x" and step.d == FWD:
                        u_ready[FWD] = start + step.n + 1
                for slot in range(SLOTS):
                    spread_du(i, slot)
                    for n in range(spread_before[slot], spread_before[slot + 1]):
                        if n < SLOTS:
                            spread_delta(i, n)
                        elif nxt is not None:
                            spread_delta(i + 1, n - SLOTS)
                    for step in steps:
                        if step.kind == "x" and slot == (X_REV if step.d else X_FWD)[step.half][0]:
                            conv_first_half(step, i, start)
                        if step.pe == slot:
                            run(step, i, start, u_ready)
                    for b in range(YB):
                        if SUM[b] == slot:
                            sum_batch(i, b)
                        elif SUM[b] == slot + SLOTS and prev is not None:
                            sum_batch(i - 1, b)
                    for e in range(4):
                        if ADD_UD[e] == slot:
                            add_ud(i, e, cur)
                    for half in range(2):
                        if ADD_FWD[half] == slot:
                            add_forward(i, half)

            def tail(i):
                for b in range(YB):
                    if SUM[b] >= SLOTS:
                        sum_batch(i - 1, b)
                at_least(pe, s_evac, tail_start(i) - 1)
                pe.wait_ge(s_gate, 2 * i)
                project(0, out_t[1][:, :], gated[:, 1, :], CH)

            over_tiles(pe, body, tail)

        @block.scalar
        def _(act):
            act.wait_ge(s_load, N_LOAD)
            for s in range(2):
                nc.scalar.activation(a_neg[s][:, :], a_neg[s][:, :], ACT.Exp).then_inc(s_exp_a, 1)

            def take(count, bank, kind, d, half, s, tile):
                act.wait_ge(s_proj, count)
                src, dst = p_bank[bank][:, :], px(half)
                if kind == "x":
                    at_least(act, s_ud, 4 * (tile - 1) + (2 if d == FWD else 4))
                    nc.scalar.activation(u[d][:, dst], src, ACT.Silu,
                                         bias=cols[s][:, 0:1]).then_inc(s_evac, 1)
                elif kind == "z":
                    at_least(act, s_gate, 2 * tile)
                    nc.scalar.activation(zs[:, dst], src, ACT.Silu).then_inc(s_evac, 1)
                elif kind == "b":
                    at_least(act, s_drive, SLOTS * (tile - 1) + UNIT * (1 + d))
                    nc.scalar.copy(b_rep[d][:, dst], src).then_inc(s_evac, 1)
                elif kind == "c":
                    at_least(act, s_read, SLOTS * (tile - 1) + UNIT * (1 + d))
                    nc.scalar.copy(c_rep[d][:, dst], src).then_inc(s_evac, 1)
                elif kind == "dt":
                    at_least(act, s_low, 2 * (2 * tile + d))
                    nc.scalar.activation(expabs[:, dst], src, ACT.Abs, bias=cols[s][:, 1:2])
                    nc.scalar.activation(vpos[:, dst], src, ACT.Relu,
                                         bias=cols[s][:, 1:2]).then_inc(s_evac, 1)
                else:
                    at_least(act, s_store, 16 * (2 * tile + half - 1))
                    nc.scalar.copy(o_sb[:, half, :], p_bank[bank][0:CH, :]).then_inc(s_evac, 1)

            def take_y_forward(i, e):
                act.wait_ge(s_ysum, YB * i + 4 * e + 4)
                at_least(act, s_yf_used, 2 * (i - 1) + 1 + e)
                nc.scalar.copy(y_fwd[:, px(e)], y_bank[:, :]).then_inc(s_yf, 1)

            def softplus(unit, evac, step):
                if step == 0:
                    act.wait_ge(s_evac, evac)
                    nc.scalar.activation(expabs[:, :], expabs[:, :], ACT.Exp,
                                         scale=-1.0).then_inc(s_soft, 1)
                elif step == 1:
                    act.wait_ge(s_soft, 3 * unit + 1)
                    at_least(act, s_ln, unit)
                    nc.scalar.activation(onep[:, :], expabs[:, :], ACT.Identity,
                                         bias=1.0).then_inc(s_soft, 1)
                else:
                    act.wait_ge(s_soft, 3 * unit + 1)
                    nc.scalar.activation(delta[:, :], expabs[:, :], ACT.Ln,
                                         bias=1.0).then_inc(s_soft, 1)

            def high(unit, d, t):
                act.wait_ge(s_delta, 3 * unit + 2 + t)
                at_least(act, s_stack, 16 * STACK_DMAS * unit)
                if t == 0:
                    nc.scalar.copy(inner(d_parts[d][:, 0, :], d), inner(delta[:, :], d)).then_inc(s_hi, 1)
                else:
                    nc.scalar.copy(u_parts[:, 0, :], du[:, :]).then_inc(s_hi, 1)

            def middle(unit, d, t):
                act.wait_ge(s_rest, 2 * unit + 1 + t)
                if t == 0:
                    nc.scalar.copy(inner(d_parts[d][:, 1, :], d), inner(delta[:, :], d)).then_inc(s_mid, 1)
                else:
                    nc.scalar.copy(u_parts[:, 1, :], du[:, :]).then_inc(s_mid, 1)

            act.wait_ge(s_prep, 4)
            act.preload_act_table_set("natural_log_exp_and_others")
            for n, (kind, d, h) in enumerate(BEFORE):
                take(n + 1, n % 2, kind, d, h, 0, 0)
            for step in range(3):
                softplus(0, 4, step)
            for f in (high, middle):
                for t in range(2):
                    f(0, FWD, t)

            def body(i, cur, prev, nxt):
                start = steps_before(i, prev is None)
                steps = plan(prev, cur, nxt)
                dt1 = {step.d: start + step.n + 1 for step in steps if step.kind == "dt"}
                units = [(0, 2 * i + 1, REV)] + ([(UNIT, 2 * i + 2, FWD)] if nxt is not None else [])
                for slot in range(SLOTS):
                    d, half, k, j = group_of(slot)
                    g = SLOTS * i + slot
                    act.wait_ge(s_delta_b, g + 1)
                    at_least(act, s_state, g - A_RING + 1)
                    nc.scalar.activation(inner(decay[d][:, slot % A_RING, :], d),
                                         inner(d_bank[slot % 2][:, :], d), ACT.Exp,
                                         scale=a_neg[cur][:, 4 * j + k:4 * j + k + 1]).then_inc(s_decay, 1)
                    if slot == SILU_REV and prev is not None:
                        for h in range(2):
                            take(start - 1 + h, h, "x", REV, h, cur, i)
                    for step in steps:
                        if step.act == slot:
                            tile = {"x": i + 1, "z": i, "out": i - step.half}.get(
                                step.kind, i if step.d == REV else i + 1)
                            take(start + step.n + 1, step.bank, step.kind, step.d, step.half,
                                 step.weights, tile)
                    if slot in (SILU_Z, SILU_FWD) or slot == SILU_REV and prev is not None:
                        act.preload_act_table_set("natural_log_exp_and_others")
                    if slot in TAKE_FWD:
                        take_y_forward(i, TAKE_FWD.index(slot))
                    for at, unit, du_dir in units:
                        for step in range(3):
                            if slot == at + SOFTPLUS[step]:
                                softplus(unit, dt1[du_dir], step)
                        if slot - at in HIGH:
                            high(unit, du_dir, HIGH.index(slot - at))
                        if slot - at in MIDDLE:
                            middle(unit, du_dir, MIDDLE.index(slot - at))

            def tail(i):
                take(tail_start(i) + 1, 0, "out", REV, 1, 1, i - 1)

            over_tiles(act, body, tail)

        @block.vector
        def _(dve):
            nc.vector.memset(xt[:, :, :], 0.0).then_inc(s_prep, 1)
            for d in range(2):
                for part in range(3):
                    ins = nc.vector.memset(first(d_parts[d][:, part, :], d), 0.0)
                ins = nc.vector.memset(decay[d][:, :, :], 0.0)
            ins.then_inc(s_prep, 1)
            dve.wait_ge(s_load, N_LOAD)
            nc.vector.tensor_copy(spread[0:96, :, :],
                                  sel_f[0:96, 0:4 * P].rearrange("p (k m) -> p k m", k=4))
            for s in range(2):
                tap = taps[s]
                w = in_t[s][:, 0:DI]
                nc.vector.tensor_tensor(tap[:, :, :], tap[:, :, :],
                                        w.unsqueeze(1).broadcast_to([P, 4, DI]), ALU.mult)
                for dst, c0 in ((to_b[s], DTR), (to_c[s], DTR + NS)):
                    nc.vector.tensor_copy(dst[:, :].rearrange("p (n r) -> p n r", r=8),
                                          xp_t[s][:, c0:c0 + NS].unsqueeze(2).broadcast_to([P, NS, 8]))
                nc.vector.tensor_scalar(d_diag[s][:, :], sel_f[:, 5 * P:6 * P], cols[s][:, 2:3], None,
                                        ALU.mult)
                dve.wait_ge(s_dtw, s + 1)
                nc.vector.tensor_copy(to_dt[s][:, :], p_bank[s][:, 0:P])
                dve.wait_ge(s_exp_a, s + 1)
                nc.vector.tensor_scalar(a_neg[s][:, :], a_neg[s][:, :], -1.0, None,
                                        ALU.mult).then_inc(s_prep, 1)

            def correction(unit):
                dve.wait_ge(s_soft, 3 * unit + 3)
                nc.vector.scalar_tensor_tensor(out=onep[:, :], in0=onep[:, :], scalar=-1.0,
                                               in1=expabs[:, :], op0=ALU.add,
                                               op1=ALU.subtract).then_inc(s_delta, 1)

            def finish_delta(unit):
                dve.wait_ge(s_ln, unit + 1)
                nc.vector.tensor_tensor(delta[:, :], delta[:, :], vpos[:, :],
                                        ALU.add).then_inc(s_delta, 1)

            def finish_du(unit, d):
                dve.wait_ge(s_delta, 3 * unit + 2)
                nc.vector.tensor_tensor(du[:, :], delta[:, :], u[d][:, :], ALU.mult).then_inc(s_delta, 1)

            def rest(unit, d, t):
                dve.wait_ge(s_hi, 2 * unit + 1 + t)
                dve.wait_ge(s_delta, 3 * unit + 3)
                src = (delta, du)[t]
                if t == 0:
                    src, hi = inner(delta[:, :], d), inner(d_parts[d][:, 0, :], d)
                else:
                    src, hi = du[:, :], u_parts[:, 0, :]
                nc.vector.tensor_tensor(src, src, hi, ALU.subtract).then_inc(s_rest, 1)

            def make_drive(i, slot):
                d, half, k, j = group_of(slot)
                bank = u_bank[slot % UNIT % 3]
                dve.wait_ge(s_du_b, SLOTS * i + slot + 1)
                nc.vector.tensor_tensor(bank[:, :], bank[:, :], b_rep[d][:, px(half)],
                                        ALU.mult).then_inc(s_drive, 1)

            def scan(i, slot):
                d, half, k, j = group_of(slot)
                g = SLOTS * i + slot
                dve.wait_ge(s_decay, g + 1)
                dve.wait_ge(s_drive, g + 1)
                at_least(dve, s_read, g - H_RING + 1)
                step = 1 if d == FWD else -1
                nc.vector.tensor_tensor_scan(state[:, slot % H_RING, ::step],
                                             decay[d][:, slot % A_RING, ::step],
                                             u_bank[slot % UNIT % 3][:, ::step], 0.0,
                                             ALU.mult, ALU.add).then_inc(s_state, 1)

            def gate(i, half, projected):
                dve.wait_ge(s_ysum, YB * i + 4 * (2 + half) + 4)
                at_least(dve, s_proj, projected)
                nc.vector.tensor_tensor(gated[:, half, :], y_bank[:, :], zs[:, px(half)],
                                        ALU.mult).then_inc(s_gate, 1)

            correction(0)
            finish_delta(0)
            finish_du(0, FWD)
            for t in range(2):
                rest(0, FWD, t)

            def body(i, cur, prev, nxt):
                start = steps_before(i, prev is None)
                units = [(0, 2 * i + 1, REV)] + ([(UNIT, 2 * i + 2, FWD)] if nxt is not None else [])
                for slot in range(SLOTS):
                    make_drive(i, slot)
                    if slot > 0:
                        scan(i, slot - 1)
                    elif prev is not None:
                        scan(i - 1, SLOTS - 1)
                    if slot == GATE_1 and prev is not None:
                        gate(i - 1, 1, start + 6 - STEPS + 1)
                    if slot == GATE_0:
                        gate(i, 0, start)
                    for at, unit, d in units:
                        if slot == at + CORRECT:
                            correction(unit)
                        if slot == at + DELTA_AT:
                            finish_delta(unit)
                        if slot == at + DU_AT:
                            finish_du(unit, d)
                        if slot - at in REST:
                            rest(unit, d, REST.index(slot - at))

            def tail(i):
                scan(i - 1, SLOTS - 1)
                gate(i - 1, 1, steps_before(i - 1, False) + 7)

            over_tiles(dve, body, tail)

        @block.gpsimd
        def _(pool):
            def low(unit, d, t):
                pool.wait_ge(s_mid, 2 * unit + 1 + t)
                if t == 0:
                    nc.gpsimd.tensor_tensor(inner(d_parts[d][:, 2, :], d), inner(delta[:, :], d),
                                            inner(d_parts[d][:, 1, :], d), ALU.subtract).then_inc(s_low, 1)
                else:
                    nc.gpsimd.tensor_tensor(u_parts[:, 2, :], du[:, :], u_parts[:, 1, :],
                                            ALU.subtract).then_inc(s_low, 1)

            def correct_log(unit):
                pool.wait_ge(s_delta, 3 * unit + 1)
                nc.gpsimd.tensor_tensor(delta[:, :], delta[:, :], onep[:, :],
                                        ALU.subtract).then_inc(s_ln, 1)

            correct_log(0)
            for t in range(2):
                low(0, FWD, t)

            def body(i, cur, prev, nxt):
                units = [(0, 2 * i + 1, REV)] + ([(UNIT, 2 * i + 2, FWD)] if nxt is not None else [])
                for slot in range(SLOTS):
                    d, half, k, j = group_of(slot)
                    pool.wait_ge(s_state, SLOTS * i + slot + 1)
                    at_least(pool, s_ysum, YB * i + slot // 4 - C_RING // 4 + 1)
                    nc.gpsimd.tensor_tensor(read[:, slot % C_RING, :], state[:, slot % H_RING, :],
                                            c_rep[d][:, px(half)], ALU.mult).then_inc(s_read, 1)
                    for at, unit, du_dir in units:
                        if slot == at + LOG:
                            correct_log(unit)
                        if slot - at in LOW:
                            low(unit, du_dir, LOW.index(slot - at))

            over_tiles(pool, body, lambda i: None)


def both_halves(dram_image):
    v = dram_image.rearrange("n c (h p) -> h (n c) p", h=2)
    return v[0], v[1]


def norm_stage(nc, xs, rec, x2, gn, consts):
    with ExitStack() as ctx:
        def sb(name, shape, dt=F32):
            return ctx.enter_context(nc.sbuf_tensor(name, shape, dt))

        def sem(name):
            return ctx.enter_context(nc.semaphore(name))

        HP = SIDE * SIDE // 2
        rows = [sb(f"n_rows{n}", [P, HP]) for n in range(2)]
        res = [sb(f"n_res{n}", [P, HP]) for n in range(2)]
        colp = sb("n_cols", [P, HP])
        stats = sb("n_stats", [P, HP // HALF, 6])
        mv = sb("n_mv", [P, 2])
        ms = sb("n_ms", [P, 2])
        gm = sb("n_gm", [P, 2])
        nv = sb("n_nv", [P, 1])
        sd = sb("n_sd", [P, 1])
        rs = sb("n_rs", [P, 1])
        scale = sb("n_scale", [P, 2])
        ma = sb("n_ma", [P, 2])
        shift = sb("n_shift", [P, 2])
        gnt = sb("n_gn", [P, 2])
        avg = sb("n_avg", [P, P])
        mean_ps = ctx.enter_context(nc.psum_tensor("n_mean", [P, 2], F32))

        s_w = sem("gn_weights_loaded")
        s_rowx = [sem("norm_rows_loaded0"), sem("norm_rows_loaded1")]
        s_col = sem("norm_cols_loaded")
        s_sum = sem("norm_summed")
        s_bn = sem("norm_chain")
        s_mean = sem("norm_group_mean")
        s_shift = sem("norm_affine_ready")
        s_sd = sem("norm_root")
        s_act = sem("norm_silu")
        s_res = sem("norm_residual")
        s_out = sem("norm_stored")
        CHAIN = 9

        block = ctx.enter_context(nc.Block())

        def over_images(engine, image):
            for b in range(BATCH):
                image(b, b % 2)

        @block.sync
        def _(sp):
            sp.dma_start(gnt[:, :], gn).then_inc(s_w, 16)
            sp.dma_start(avg[:, :], consts[:, 0:P]).then_inc(s_w, 16)

            def load(b, n):
                at_least(sp, s_out, 32 * (b - 1))
                for src, dst in ((rec, rows[n]), (xs, res[n])):
                    for h in range(2):
                        sp.dma_start(dst[64 * h:64 * h + 64, :].rearrange("c (t p) -> c t p", p=PX),
                                     src[bass.ds(b * 16 + 8 * h, 8)].rearrange("t c p -> c t p")
                                     ).then_inc(s_rowx[n], 16)
                at_least(sp, s_sum, b)
                for h in range(2):
                    dst = colp[64 * h:64 * h + 64, :].rearrange("c (t r p) -> c t r p", r=SEQS, p=64)
                    src = rec[bass.ds(TILES + b * 16, 16)].rearrange("t c (r p) -> c t r p", p=SIDE)
                    for t in range(16):
                        sp.dma_start(dst[:, t], src[:, t, :, 64 * h:64 * h + 64]).then_inc(s_col, 16)

            def store(b, n):
                sp.wait_ge(s_res, b + 1)
                for h, dst in enumerate(both_halves(x2[bass.ds(b, 1)])):
                    sp.dma_start(dst, res[n][64 * h:64 * h + 64, :]).then_inc(s_out, 16)

            load(0, 0)
            load(1, 1)
            for b in range(BATCH):
                store(b, b % 2)
                if b + 2 < BATCH:
                    load(b + 2, b % 2)
            sp.wait_ge(s_out, 32 * BATCH)

        @block.vector
        def _(dve):
            def image(b, n):
                c = CHAIN * b
                dve.wait_ge(s_rowx[n], 32 * (b - n) + 64)
                dve.wait_ge(s_col, 16 * 32 * (b + 1))
                nc.vector.tensor_tensor(rows[n][:, :].rearrange("p (h w) -> p h w", w=SIDE),
                                        rows[n][:, :].rearrange("p (h w) -> p h w", w=SIDE),
                                        colp[:, :].rearrange("p (w h) -> p h w", w=SIDE),
                                        ALU.add).then_inc(s_sum, 1)
                dve.wait_ge(s_sum, b + 1)
                for t in range(HP // HALF):
                    ins = nc.vector.bn_stats(stats[:, t, :], rows[n][:, t * HALF:(t + 1) * HALF])
                ins.then_inc(s_bn, 1)
                dve.wait_ge(s_bn, c + 1)
                nc.vector.bn_aggr(mv[:, :], stats[:, :, :]).then_inc(s_bn, 1)
                dve.wait_ge(s_bn, c + 2)
                nc.vector.tensor_copy(ms[:, 0:1], mv[:, 0:1])
                nc.vector.scalar_tensor_tensor(out=ms[:, 1:2], in0=mv[:, 0:1], scalar=mv[:, 0:1],
                                               in1=mv[:, 1:2], op0=ALU.mult, op1=ALU.add).then_inc(s_bn, 1)
                dve.wait_ge(s_mean, b + 1)
                nc.vector.tensor_copy(gm[:, :], mean_ps[:, :]).then_inc(s_bn, 1)
                dve.wait_ge(s_bn, c + 4)
                nc.vector.scalar_tensor_tensor(out=nv[:, :], in0=gm[:, 0:1], scalar=gm[:, 0:1],
                                               in1=gm[:, 1:2], op0=ALU.mult, op1=ALU.subtract).then_inc(s_bn, 1)
                dve.wait_ge(s_bn, c + 5)
                nc.vector.tensor_scalar(nv[:, :], nv[:, :], -1.0 / 16, EPS, ALU.mult,
                                        ALU.add).then_inc(s_bn, 1)
                dve.wait_ge(s_sd, b + 1)
                nc.vector.reciprocal(rs[:, :], sd[:, :]).then_inc(s_bn, 1)
                dve.wait_ge(s_bn, c + 7)
                at_least(dve, s_act, b - 1)
                nc.vector.scalar_tensor_tensor(out=scale[:, n:n + 1], in0=rs[:, :], scalar=0.25,
                                               in1=gnt[:, 0:1], op0=ALU.mult, op1=ALU.mult).then_inc(s_bn, 1)
                dve.wait_ge(s_bn, c + 8)
                nc.vector.tensor_tensor(ma[:, n:n + 1], gm[:, 0:1], scale[:, n:n + 1],
                                        ALU.mult).then_inc(s_bn, 1)
                dve.wait_ge(s_bn, c + 9)
                nc.vector.tensor_tensor(shift[:, n:n + 1], gnt[:, 1:2], ma[:, n:n + 1],
                                        ALU.subtract).then_inc(s_shift, 1)
                dve.wait_ge(s_act, b + 1)
                nc.vector.tensor_tensor(res[n][:, :], res[n][:, :], rows[n][:, :],
                                        ALU.add).then_inc(s_res, 1)
            dve.wait_ge(s_w, 32)
            over_images(dve, image)

        @block.tensor
        def _(pe):
            pe.wait_ge(s_w, 32)

            def image(b, n):
                pe.wait_ge(s_bn, CHAIN * b + 3)
                nc.tensor.matmul(mean_ps[:, :], avg[:, :], ms[:, :], start=True,
                                 stop=True).then_inc(s_mean, 1)
            over_images(pe, image)

        @block.scalar
        def _(act):
            def image(b, n):
                act.wait_ge(s_bn, CHAIN * b + 6)
                nc.scalar.activation(sd[:, :], nv[:, :], ACT.Sqrt).then_inc(s_sd, 1)
                act.wait_ge(s_shift, b + 1)
                nc.scalar.activation(rows[n][:, :], rows[n][:, :], ACT.Silu, bias=shift[:, n:n + 1],
                                     scale=scale[:, n:n + 1]).then_inc(s_act, 1)
            over_images(act, image)


def weight_stage(nc, p_weight, origin, new_param, consts, w_conv):
    CO = 8
    CHUNK = CO * CH * KTAPS
    CHUNKS = KSIZE // CHUNK
    with ExitStack() as ctx:
        def sb(name, shape, dt=F32):
            return ctx.enter_context(nc.sbuf_tensor(name, shape, dt))

        def sem(name):
            return ctx.enter_context(nc.semaphore(name))

        keys = [sb(f"w_keys{n}", [KEYS + 1, CHUNK]) for n in range(2)]
        par = sb("w_par", [KEYS + 1, 2])
        raw = sb("w_raw", [P, 2 * CHUNKS, CO // 2, KTAPS])
        made = [ctx.enter_context(nc.psum_tensor(f"w_made{n}", [P, HALF], F32)) for n in range(2)]
        s_par = sem("param_loaded")
        s_keys = [sem("keys_loaded0"), sem("keys_loaded1")]
        s_made = sem("weights_made")
        s_raw = sem("weights_copied")
        s_laid = sem("weights_laid_out")
        block = ctx.enter_context(nc.Block())

        def over_chunks(engine, chunk):
            chunk(0, 0, 0)
            chunk(1, 1, 0)
            with engine.Fori(1, CHUNKS // 2) as i:
                for n in range(2):
                    chunk(2 * i + n, n, 0)
            with engine.Fori(CHUNKS // 2, CHUNKS) as i:
                for n in range(2):
                    chunk(2 * i + n, n, 1)

        @block.sync
        def _(sp):
            for c in range(2):
                sp.dma_start(par[0:KEYS, c:c + 1], new_param).then_inc(s_par, 16)
            sp.dma_start(par[KEYS:KEYS + 1, 0:1], consts[0:1, 2 * P:2 * P + 1]).then_inc(s_par, 16)
            sp.dma_start(par[KEYS:KEYS + 1, 1:2], new_param[KEYS - 1:KEYS, :]).then_inc(s_par, 16)

            def chunk(m, n, c):
                at_least(sp, s_made, m - 1)
                at = bass.ds(m * CHUNK, CHUNK)
                sp.dma_start(keys[n][0:KEYS, :], p_weight[:, at]).then_inc(s_keys[n], 16)
                sp.dma_start(keys[n][KEYS:KEYS + 1, :], origin[:, at]).then_inc(s_keys[n], 16)
            over_chunks(sp, chunk)

        @block.tensor
        def _(pe):
            pe.wait_ge(s_par, 64)

            def chunk(m, n, c):
                pe.wait_ge(s_keys[n], 16 * (m - n) + 32)
                at_least(pe, s_raw, m - 1)
                k = keys[n][:, :].rearrange("k (o q i t) -> k o t q i", q=2, i=CH, t=KTAPS)
                for o in range(CO // 2):
                    for t in range(KTAPS):
                        col = o * KTAPS + t
                        mm = nc.tensor.matmul(made[n][:, col:col + 1], k[:, o, t], par[:, c:c + 1],
                                              start=True, stop=True)
                mm.then_inc(s_made, 1)
            over_chunks(pe, chunk)

        @block.vector
        def _(dve):
            for c in range(2):
                nc.vector.memset(w_conv[c][:, :, :], 0.0).then_inc(s_laid, 1)

            def chunk(m, n, c):
                dve.wait_ge(s_made, m + 1)
                nc.vector.tensor_copy(raw[:, bass.ds(m, 1), :, :].rearrange("p m o t -> p (m o t)"),
                                      made[n][:, 0:CO // 2 * KTAPS]).then_inc(s_raw, 1)
            over_chunks(dve, chunk)
            dve.wait_ge(s_raw, 2 * CHUNKS)
            dve.wait_ge(s_laid, 2)
            for c in range(2):
                for q in range(2):
                    src = raw[64 * q:64 * q + 64, c * CHUNKS:(c + 1) * CHUNKS].rearrange(
                        "p m o t -> p t (m o)")
                    for dy, rows, m0 in ((0, 0, 0), (1, 64, 0), (2, 0, 3)):
                        dst = w_conv[c][rows:rows + 64, m0:m0 + 3, :].rearrange(
                            "p d (o q) -> p d o q", q=2)[:, :, :, q]
                        nc.vector.tensor_copy(dst, src[:, 3 * dy:3 * dy + 3, :]).then_inc(s_laid, 1)
            dve.wait_ge(s_laid, 14)


def conv_stage(nc, tag, src, dst, w, affine, bn, consts, out_affine):
    with ExitStack() as ctx:
        def sb(name, shape, dt=F32):
            return ctx.enter_context(nc.sbuf_tensor(f"{tag}_{name}", shape, dt))

        def sem(name):
            return ctx.enter_context(nc.semaphore(f"{tag}_{name}"))

        W = SIDE + 2
        BLOCKS = 16
        img = [sb(f"img{n}", [P, W, W]) for n in range(2)]
        out = sb("out", [P, 2, 4 * HALF])
        stats = sb("stats", [P, BATCH * BLOCKS, 6])
        mv = sb("mv", [P, 2])
        ms = sb("ms", [P, 2])
        gm = sb("gm", [P, 2])
        nv = sb("nv", [P, 1])
        sd = sb("sd", [P, 1])
        rs = sb("rs", [P, 1])
        ma = sb("ma", [P, 1])
        bnt = sb("bn", [P, 2])
        avg = sb("avg", [P, P])
        acc = [ctx.enter_context(nc.psum_tensor(f"{tag}_acc{n}", [P, HALF], F32)) for n in range(8)]

        s_w = sem("weights_loaded")
        s_zero = sem("borders_zero")
        s_img = [sem("image_loaded0"), sem("image_loaded1")]
        s_pre = sem("image_activated")
        s_conv = sem("block_convolved")
        s_copy = sem("block_copied")
        s_stat = sem("block_measured")
        s_out = [sem("quarter_stored0"), sem("quarter_stored1")]
        s_chain = sem("chain")
        s_mean = sem("mean")
        s_sd = sem("root")
        block = ctx.enter_context(nc.Block())

        def over_images(engine, image):
            image(0, 0)
            image(1, 1)
            with engine.Fori(1, BATCH // 2) as i:
                image(2 * i, 0)
                image(2 * i + 1, 1)

        def body_of(n, half):
            rows = slice(1, 1 + SIDE) if half == 0 else slice(0, SIDE)
            return img[n][64 * half:64 * half + 64, rows, 1:1 + SIDE]

        @block.sync
        def _(sp):
            sp.dma_start(bnt[:, :], bn).then_inc(s_w, 16)
            sp.dma_start(avg[:, :], consts[:, P:2 * P]).then_inc(s_w, 16)
            sp.wait_ge(s_zero, 2)

            def load(b, n):
                at_least(sp, s_conv, BLOCKS * (b - 1))
                for half in range(2):
                    sp.dma_start(body_of(n, half),
                                 src[bass.ds(b, 1)].rearrange("n c (h w) -> (n c) h w", w=SIDE)
                                 ).then_inc(s_img[n], 16)

            def store(b):
                for q in range(4):
                    sp.wait_ge(s_copy, BLOCKS * b + 4 * q + 4)
                    sp.wait_ge(s_stat, BLOCKS * b + 4 * q + 4)
                    for h, half in enumerate(both_halves(dst[bass.ds(b, 1)])):
                        sp.dma_start(half[:, 4 * q * HALF:4 * (q + 1) * HALF],
                                     out[64 * h:64 * h + 64, q % 2, :]).then_inc(s_out[q % 2], 16)

            load(0, 0)
            load(1, 1)
            with sp.Fori(0, BATCH // 2 - 1) as i:
                for n in range(2):
                    store(2 * i + n)
                    load(2 * i + 2 + n, n)
            store(BATCH - 2)
            store(BATCH - 1)
            for n in range(2):
                sp.wait_ge(s_out[n], 64 * BATCH)

        @block.tensor
        def _(pe):
            pe.wait_ge(s_w, 32)

            def image(b, n):
                if affine is None:
                    pe.wait_ge(s_img[n], 16 * (b - n) + 32)
                else:
                    pe.wait_ge(s_pre, 2 * b + 2)
                for m in range(BLOCKS):
                    at_least(pe, s_copy, BLOCKS * b + m - 7)
                    for t in range(6):
                        dy, dx = (0, t) if t < 3 else (2, t - 3)
                        for h in range(2):
                            y = 64 * h + 4 * m + dy
                            mm = nc.tensor.matmul(acc[m % 8][64 * h:64 * h + 64, :], w[:, t, :],
                                                  img[n][:, y:y + 4, dx:dx + SIDE],
                                                  start=(t == 0), stop=(t == 5),
                                                  tile_position=(0, 64 * h))
                    mm.then_inc(s_conv, 1)
            over_images(pe, image)
            pe.wait_ge(s_chain, 3)
            nc.tensor.matmul(acc[0][:, 0:2], avg[:, :], ms[:, :], start=True, stop=True).then_inc(s_mean, 1)

        @block.scalar
        def _(act):
            def activate(b, n):
                if affine is None:
                    return
                act.wait_ge(s_img[n], 16 * (b - n) + 32)
                for half in range(2):
                    v = body_of(n, half)
                    rows = slice(64 * half, 64 * half + 64)
                    nc.scalar.activation(v, v, ACT.Relu, bias=affine[rows, 1:2],
                                         scale=affine[rows, 0:1]).then_inc(s_pre, 1)

            def image(b, n):
                for m in range(BLOCKS):
                    if m == 4:
                        later(b + 1, 1 - n)
                    act.wait_ge(s_conv, BLOCKS * b + m + 1)
                    if m % 4 == 0:
                        at_least(act, s_out[m // 4 % 2], 64 * b + 32 * (m // 8))
                    nc.scalar.copy(out[:, m // 4 % 2, (m % 4) * HALF:(m % 4 + 1) * HALF],
                                   acc[m % 8][:, :]).then_inc(s_copy, 1)

            later = activate
            activate(0, 0)
            image(0, 0)
            image(1, 1)
            with act.Fori(1, BATCH // 2 - 1) as i:
                image(2 * i, 0)
                image(2 * i + 1, 1)
            image(BATCH - 2, 0)
            later = lambda b, n: None
            image(BATCH - 1, 1)
            act.wait_ge(s_chain, 6)
            nc.scalar.activation(sd[:, :], nv[:, :], ACT.Sqrt).then_inc(s_sd, 1)

        @block.vector
        def _(dve):
            for n in range(2):
                nc.vector.memset(img[n][:, :, :], 0.0).then_inc(s_zero, 1)
            dve.wait_ge(s_w, 32)

            def image(b, n):
                for m in range(BLOCKS):
                    dve.wait_ge(s_copy, BLOCKS * b + m + 1)
                    nc.vector.bn_stats(stats[:, bass.ds(b * BLOCKS + m, 1), :].rearrange("p o s -> p (o s)"),
                                       out[:, m // 4 % 2, (m % 4) * HALF:(m % 4 + 1) * HALF]
                                       ).then_inc(s_stat, 1)
            over_images(dve, image)
            dve.wait_ge(s_stat, BATCH * BLOCKS)
            nc.vector.bn_aggr(mv[:, :], stats[:, :, :]).then_inc(s_chain, 1)
            dve.wait_ge(s_chain, 1)
            nc.vector.tensor_copy(ms[:, 0:1], mv[:, 0:1]).then_inc(s_chain, 1)
            nc.vector.scalar_tensor_tensor(out=ms[:, 1:2], in0=mv[:, 0:1], scalar=mv[:, 0:1],
                                           in1=mv[:, 1:2], op0=ALU.mult, op1=ALU.add).then_inc(s_chain, 1)
            dve.wait_ge(s_mean, 1)
            nc.vector.tensor_copy(gm[:, :], acc[0][:, 0:2]).then_inc(s_chain, 1)
            dve.wait_ge(s_chain, 4)
            nc.vector.scalar_tensor_tensor(out=nv[:, :], in0=gm[:, 0:1], scalar=gm[:, 0:1],
                                           in1=gm[:, 1:2], op0=ALU.mult, op1=ALU.subtract).then_inc(s_chain, 1)
            dve.wait_ge(s_chain, 5)
            nc.vector.tensor_scalar(nv[:, :], nv[:, :], -1.0, EPS, ALU.mult, ALU.add).then_inc(s_chain, 1)
            dve.wait_ge(s_sd, 1)
            nc.vector.reciprocal(rs[:, :], sd[:, :]).then_inc(s_chain, 1)
            dve.wait_ge(s_chain, 7)
            nc.vector.tensor_tensor(out_affine[:, 0:1], rs[:, :], bnt[:, 0:1], ALU.mult).then_inc(s_chain, 1)
            dve.wait_ge(s_chain, 8)
            nc.vector.tensor_tensor(ma[:, :], gm[:, 0:1], out_affine[:, 0:1], ALU.mult).then_inc(s_chain, 1)
            dve.wait_ge(s_chain, 9)
            nc.vector.tensor_tensor(out_affine[:, 1:2], bnt[:, 1:2], ma[:, :], ALU.subtract).then_inc(s_chain, 1)
            dve.wait_ge(s_chain, 10)


def end_stage(nc, y2, x2, out, affine):
    with ExitStack() as ctx:
        def sem(name):
            return ctx.enter_context(nc.semaphore(name))

        HP = SIDE * SIDE // 2
        y = [ctx.enter_context(nc.sbuf_tensor(f"e_y{n}", [P, HP], F32)) for n in range(2)]
        x = [ctx.enter_context(nc.sbuf_tensor(f"e_x{n}", [P, HP], F32)) for n in range(2)]
        s_in = [sem("end_loaded0"), sem("end_loaded1")]
        s_add = sem("end_added")
        s_relu = sem("end_relu")
        s_out = sem("end_stored")
        block = ctx.enter_context(nc.Block())

        def over_images(engine, image):
            image(0, 0)
            image(1, 1)
            with engine.Fori(1, BATCH // 2) as i:
                image(2 * i, 0)
                image(2 * i + 1, 1)

        @block.sync
        def _(sp):
            def load(b, n):
                at_least(sp, s_out, 32 * (b - 1))
                for src, dst in ((y2, y[n]), (x2, x[n])):
                    for h, half in enumerate(both_halves(src[bass.ds(b, 1)])):
                        sp.dma_start(dst[64 * h:64 * h + 64, :], half).then_inc(s_in[n], 16)

            def store(b, n):
                sp.wait_ge(s_relu, b + 1)
                for h, half in enumerate(both_halves(out[bass.ds(b, 1)])):
                    sp.dma_start(half, y[n][64 * h:64 * h + 64, :]).then_inc(s_out, 16)

            load(0, 0)
            load(1, 1)
            with sp.Fori(0, BATCH // 2 - 1) as i:
                for n in range(2):
                    store(2 * i + n, n)
                    load(2 * i + 2 + n, n)
            store(BATCH - 2, 0)
            store(BATCH - 1, 1)
            sp.wait_ge(s_out, 32 * BATCH)

        @block.vector
        def _(dve):
            def image(b, n):
                dve.wait_ge(s_in[n], 32 * (b - n) + 64)
                nc.vector.scalar_tensor_tensor(out=y[n][:, :], in0=y[n][:, :], scalar=affine[:, 0:1],
                                               in1=x[n][:, :], op0=ALU.mult, op1=ALU.add).then_inc(s_add, 1)
            over_images(dve, image)

        @block.scalar
        def _(act):
            def image(b, n):
                act.wait_ge(s_add, b + 1)
                nc.scalar.activation(y[n][:, :], y[n][:, :], ACT.Relu, bias=affine[:, 1:2]).then_inc(s_relu, 1)
            over_images(act, image)


def build(nc, a, out):
    sets = [{k: a[f"{k}_{s}"] for k in ("in_t", "conv_t", "xp_t", "xp_dt", "dt_t", "out_t", "a_log", "cols")}
            for s in ("row", "col")]
    rec = nc.dram_tensor("rec", (2 * TILES, CH, PX), F32, kind="Internal").ap()
    x2 = nc.dram_tensor("x2", (BATCH, CH, SIDE * SIDE), F32, kind="Internal").ap()
    y1 = nc.dram_tensor("y1", (BATCH, CH, SIDE * SIDE), F32, kind="Internal").ap()
    y2 = nc.dram_tensor("y2", (BATCH, CH, SIDE * SIDE), F32, kind="Internal").ap()
    scan_stage(nc, a["xs"], rec, sets, a["select"])
    norm_stage(nc, a["xs"], rec, x2, a["gn"], a["average"])
    with ExitStack() as ctx:
        w_conv = [ctx.enter_context(nc.sbuf_tensor(f"w_conv{c}", [P, 6, CH], F32)) for c in range(2)]
        affine = [ctx.enter_context(nc.sbuf_tensor(f"affine{c}", [P, 2], F32)) for c in range(2)]
        weight_stage(nc, a["p_weight"], a["origin"], a["new_param"], a["average"], w_conv)
        conv_stage(nc, "c1", x2, y1, w_conv[0], None, a["bn1"], a["average"], affine[0])
        conv_stage(nc, "c2", y1, y2, w_conv[1], affine[0], a["bn2"], a["average"], affine[1])
        end_stage(nc, y2, x2, out, affine[1])


def kernel(**inputs):
    import numpy as np
    import concourse.bacc as bacc
    from concourse.bass_utils import run_bass_kernel_spmd

    def arr(name):
        return np.asarray(inputs[name])

    def tiles_of(x):
        return x.reshape(BATCH, CH, SIDE // SEQS, SEQS, SIDE).transpose(0, 2, 1, 3, 4).reshape(-1, CH, PX)

    x = arr("x")
    arrays = {"xs": np.concatenate([tiles_of(x), tiles_of(x.transpose(0, 1, 3, 2))])}
    for s in ("row", "col"):
        w = {k: arr(f"L0_conv_{s}_{k}") for k in
             ("in_w", "conv_w", "conv_b", "xp_w", "dt_w", "dt_b", "A_log", "D", "out_w")}
        arrays[f"in_t_{s}"] = w["in_w"].T
        arrays[f"conv_t_{s}"] = w["conv_w"][:, 0, :].T
        arrays[f"xp_t_{s}"] = w["xp_w"].T
        arrays[f"xp_dt_{s}"] = w["xp_w"][:DTR]
        arrays[f"dt_t_{s}"] = w["dt_w"].T
        arrays[f"out_t_{s}"] = w["out_w"].T
        arrays[f"a_log_{s}"] = w["A_log"].reshape(GROUPS, 8, NS).transpose(2, 1, 0).reshape(P, GROUPS)
        arrays[f"cols_{s}"] = np.stack([w["conv_b"], w["dt_b"], w["D"]], 1)
    twice = lambda p, q: np.concatenate([np.stack([arr(p), arr(q)], 1)] * 2)
    arrays["gn"] = twice("L0_conv_gn_w", "L0_conv_gn_b")
    arrays["bn1"] = twice("L1_conv_bn1_gamma", "L1_conv_bn1_beta")
    arrays["bn2"] = twice("L1_conv_bn2_gamma", "L1_conv_bn2_beta")
    arrays["p_weight"] = arr("L1_conv_P_weight")
    arrays["origin"] = arr("L1_conv_origin_weight")[None, :]
    arrays["new_param"] = arr("L1_conv_new_param")[:, None]

    select = np.zeros((P, 6 * P), np.float32)
    select[:, 5 * P:] = np.eye(P)
    for k in range(4):
        for r in range(8):
            for n in range(NS):
                for part in range(3):
                    select[32 * part + 8 * k + r, P * k + 8 * n + r] = 1
                select[8 * n + r, 4 * P + 32 * k + 8 * k + r] = 1
    arrays["select"] = select
    average = np.zeros((P, 2 * P + 1), np.float32)
    ch = np.arange(P) % CH
    per = CH // GN_GROUPS
    average[:, 0:P] = (ch[:, None] // per == ch[None, :] // per) / (2.0 * per)
    average[:, P:2 * P] = (ch[:, None] == ch[None, :]) / 2.0
    average[:, 2 * P] = 1
    arrays["average"] = average

    nc = bacc.Bacc("TRN2", target_bir_lowering=False, num_devices=1)
    arrays = {f"in_{k}": np.ascontiguousarray(v) for k, v in arrays.items()}
    aps = {k[3:]: nc.dram_tensor(k, v.shape, F32, kind="ExternalInput").ap() for k, v in arrays.items()}
    out = nc.dram_tensor("out", (BATCH, CH, SIDE * SIDE), F32, kind="ExternalOutput").ap()
    build(nc, aps, out)
    r = run_bass_kernel_spmd(nc, [arrays], core_ids=[0])
    return r.results[0]["out"].reshape(BATCH, CH, SIDE, SIDE)
```
